# Optimizing a Trainium2 kernel written in Bass

```python
import numpy as np
import jax
import jax.numpy as jnp

def _softmax(x, axis=-1):
    return jax.nn.softmax(x, axis=axis)

def _gelu(x):
    return jax.nn.gelu(x, approximate=True)

def _silu(x):
    return jax.nn.silu(x)

def _sigmoid(x):
    return jax.nn.sigmoid(x)

def _layernorm(x, axis=-1, eps=1e-05):
    m = jnp.mean(x, axis=axis, keepdims=True)
    v = jnp.var(x, axis=axis, keepdims=True)
    return (x - m) / jnp.sqrt(v + eps)

def _scatter_add(tgt, idx, src, axis=0):
    return tgt.at[idx].add(src)

def _segment_sum(src, seg, n):
    return jax.ops.segment_sum(src, seg, n)
kernel_name = 'mk_prb_d1_jaxref_r8_c50e51'

def setup_inputs(seed: int=0):
    np.random.seed(seed)
    _w = jnp.asarray

    def _L0_attn_setup():
        import jax, jax.numpy as jnp
        import numpy as np
        D_MODEL, N_HEADS, D_LATENT = (128, 16, 32)
        HEAD_DIM = D_MODEL // N_HEADS
        B, T = (2, 256)

        def apply_rope(x):
            Tn, D = (x.shape[1], x.shape[3])
            inv_freq = 1.0 / 10000.0 ** (jnp.arange(0, D, 2, dtype=jnp.float32) / D)
            t = jnp.arange(Tn, dtype=jnp.float32)
            freqs = jnp.outer(t, inv_freq)
            sin_f = jnp.sin(freqs)[None, :, None, :]
            cos_f = jnp.cos(freqs)[None, :, None, :]
            x1, x2 = jnp.split(x, 2, axis=-1)
            return jnp.concatenate([x1 * cos_f - x2 * sin_f, x1 * sin_f + x2 * cos_f], axis=-1)
        key = jax.random.key(seed)
        ks = jax.random.split(key, 5)
        s = lambda fan_in: 1.0 / np.sqrt(fan_in)
        return {'x': jax.random.normal(ks[0], (B, T, D_MODEL), jnp.float32), 'Wq': jax.random.normal(ks[1], (D_MODEL, D_MODEL), jnp.float32) * s(D_MODEL), 'bq': jnp.zeros((D_MODEL,), jnp.float32), 'Wkv_down': jax.random.normal(ks[2], (D_MODEL, D_LATENT), jnp.float32) * s(D_MODEL), 'bkv_down': jnp.zeros((D_LATENT,), jnp.float32), 'Wkv_up': jax.random.normal(ks[3], (D_LATENT, 2 * D_MODEL), jnp.float32) * s(D_LATENT), 'bkv_up': jnp.zeros((2 * D_MODEL,), jnp.float32), 'Wo': jax.random.normal(ks[4], (D_MODEL, D_MODEL), jnp.float32) * s(D_MODEL), 'bo': jnp.zeros((D_MODEL,), jnp.float32)}
    _L0_attn_in = _L0_attn_setup()

    def _L0_ffn_setup():
        import jax, jax.numpy as jnp
        import numpy as np
        H = 128
        E = 8
        B, S = (4, 256)
        key = jax.random.key(seed)
        k1, k2, k3, k4 = jax.random.split(key, 4)
        x = jax.random.normal(k1, (B, S, H), dtype=jnp.float32)
        wg = jax.random.normal(k2, (H, E), dtype=jnp.float32) * 0.02
        W = jax.random.normal(k3, (E, H, H), dtype=jnp.float32) * 0.02
        b = jax.random.normal(k4, (E, H), dtype=jnp.float32) * 0.02
        return {'x': x, 'wg': wg, 'W': W, 'b': b}
    _L0_ffn_in = _L0_ffn_setup()
    _d = {'L0_attn_x': _L0_attn_in['x'], 'L0_attn_Wq': _L0_attn_in['Wq'], 'L0_attn_bq': _L0_attn_in['bq'], 'L0_attn_Wkv_down': _L0_attn_in['Wkv_down'], 'L0_attn_bkv_down': _L0_attn_in['bkv_down'], 'L0_attn_Wkv_up': _L0_attn_in['Wkv_up'], 'L0_attn_bkv_up': _L0_attn_in['bkv_up'], 'L0_attn_Wo': _L0_attn_in['Wo'], 'L0_attn_bo': _L0_attn_in['bo'], 'L0_ffn_wg': _L0_ffn_in['wg'], 'L0_ffn_W': _L0_ffn_in['W'], 'L0_ffn_b': _L0_ffn_in['b']}
    _x0 = _d['L0_attn_x']
    _d['L0_attn_x'] = jax.random.normal(jax.random.fold_in(jax.random.key(seed), 1), (16, 256, 128), dtype=_x0.dtype)
    del _x0
    return _d

def reference(L0_attn_x, L0_attn_Wq, L0_attn_bq, L0_attn_Wkv_down, L0_attn_bkv_down, L0_attn_Wkv_up, L0_attn_bkv_up, L0_attn_Wo, L0_attn_bo, L0_ffn_wg, L0_ffn_W, L0_ffn_b):

    def _L0_attn_ref(x, Wq, bq, Wkv_down, bkv_down, Wkv_up, bkv_up, Wo, bo):
        import jax, jax.numpy as jnp
        import numpy as np
        D_MODEL, N_HEADS, D_LATENT = (128, 16, 32)
        HEAD_DIM = D_MODEL // N_HEADS
        B, T = (2, 256)

        def apply_rope(x):
            Tn, D = (x.shape[1], x.shape[3])
            inv_freq = 1.0 / 10000.0 ** (jnp.arange(0, D, 2, dtype=jnp.float32) / D)
            t = jnp.arange(Tn, dtype=jnp.float32)
            freqs = jnp.outer(t, inv_freq)
            sin_f = jnp.sin(freqs)[None, :, None, :]
            cos_f = jnp.cos(freqs)[None, :, None, :]
            x1, x2 = jnp.split(x, 2, axis=-1)
            return jnp.concatenate([x1 * cos_f - x2 * sin_f, x1 * sin_f + x2 * cos_f], axis=-1)
        Bn, Tn = (x.shape[0], x.shape[1])
        q = x @ Wq + bq
        kv = (x @ Wkv_down + bkv_down) @ Wkv_up + bkv_up
        q = q.reshape(Bn, Tn, N_HEADS, HEAD_DIM)
        kv = kv.reshape(Bn, Tn, N_HEADS, 2 * HEAD_DIM)
        k, v = jnp.split(kv, 2, axis=-1)
        q = apply_rope(q)
        k = apply_rope(k)
        q = q.transpose(0, 2, 1, 3)
        k = k.transpose(0, 2, 1, 3)
        v = v.transpose(0, 2, 1, 3)
        att = jnp.einsum('bhqd,bhkd->bhqk', q, k) / jnp.sqrt(jnp.float32(HEAD_DIM))
        idx = jnp.arange(Tn, dtype=jnp.float32)
        dist_signed = idx[:, None] - idx[None, :]
        log_sparse = -0.1 * jnp.log(jnp.abs(dist_signed) + 1.0)
        decay = jnp.exp(-jnp.maximum(dist_signed, 0.0) * 0.01)
        att = att + (log_sparse + jnp.log(decay + 1e-09))[None, None]
        att = jax.nn.softmax(att, axis=-1)
        out = jnp.einsum('bhqk,bhkd->bhqd', att, v)
        memory_k = jnp.mean(k, axis=2, keepdims=True)
        memory_v = jnp.mean(v, axis=2, keepdims=True)
        memory_scores = jnp.einsum('bhqd,bhkd->bhqk', q, memory_k)
        infini_out = jax.nn.sigmoid(memory_scores) * memory_v
        out = out + 0.2 * infini_out
        out = out.transpose(0, 2, 1, 3).reshape(Bn, Tn, D_MODEL)
        return out @ Wo + bo

    def _L0_ffn_ref(x, wg, W, b):
        import jax, jax.numpy as jnp
        import numpy as np
        H = 128
        E = 8
        B, S = (4, 256)
        Bb, Ss, Hh = x.shape
        Ee = wg.shape[1]
        T = Bb * Ss
        C = T // Ee
        xt = x.reshape(T, Hh)
        logits = xt @ wg
        probs = jax.nn.softmax(logits, axis=-1)
        idx = jnp.argmax(probs, axis=-1)
        mask = jax.nn.one_hot(idx, Ee, dtype=xt.dtype)
        locations = jnp.cumsum(mask, axis=0) - mask
        mask = mask * (locations < C).astype(xt.dtype)
        gate = jnp.sum(probs * mask, axis=-1)
        loc_s = jnp.sum(locations * mask, axis=-1).astype(jnp.int32)
        loc_oh = jax.nn.one_hot(loc_s, C, dtype=xt.dtype)
        dispatch = mask[:, :, None] * loc_oh[:, None, :]
        combine = gate[:, None, None] * dispatch
        exp_in = jnp.einsum('tec,th->ech', dispatch, xt)
        exp_out = jnp.einsum('ech,efh->ecf', exp_in, W) + b[:, None, :]
        out = jnp.einsum('tec,ecf->tf', combine, exp_out)
        return out.reshape(Bb, Ss, Hh)
    x = L0_attn_x
    xn = _layernorm(x, axis=-1)
    x = x + _L0_attn_ref(xn, L0_attn_Wq, L0_attn_bq, L0_attn_Wkv_down, L0_attn_bkv_down, L0_attn_Wkv_up, L0_attn_bkv_up, L0_attn_Wo, L0_attn_bo) + _L0_ffn_ref(xn, L0_ffn_wg, L0_ffn_W, L0_ffn_b)
    return x

_drawn_inputs = setup_inputs


def setup_inputs(seed=0):
    import zlib

    import numpy as np

    out = dict(_drawn_inputs(seed))
    spreads = {'L0_attn_bq': (0.0, 0.503),
     'L0_attn_bkv_down': (0.0, 0.1),
     'L0_attn_bkv_up': (0.0, 0.1),
     'L0_attn_bo': (0.0, 0.1)}
    factors = {'L0_ffn_b': 8.0}
    for name, (base, spread) in spreads.items():
        noise = np.random.default_rng([zlib.crc32(name.encode()), seed]).standard_normal(out[name].shape)
        drawn = base * np.exp(spread * noise) if base else spread * noise
        out[name] = jnp.asarray(drawn.astype(out[name].dtype))
    for name, factor in factors.items():
        out[name] = (out[name] * factor).astype(out[name].dtype)
    return out
```

```python
import numpy as np
import concourse.bass as bass
from concourse import mybir
from contextlib import ExitStack

B, T, D = 16, 256, 128
NH, HD = 16, 8
LAT = 32
NE = 8
P = 128
KT = T // P
NT = B * KT
NTOK = B * T
CAP = NTOK // NE
CK = 4
NCH = NT // CK
PAIRS = NH // 2
Q_STACK = ((0, 3), (1, 2), (2, 1))
K_STACK = 3, 2, 1
TERMS = 6
HROWS = TERMS * HD
SROWS = 2 * HROWS
HEADS = [0, 2, 4, 6, 1, 3, 5, 7, 8, 10, 12, 14, 9, 11, 13, 15]
DVE_HEADS = (3, 7, 11, 15)
SCALE = float(1.0 / np.sqrt(np.float32(HD)))
LN_EPS = 1e-5


def mixed_block_kernel(nc, x, wq, wqr, bq, bqr, wd, bd, wk, wkr, wv, wo, bo, wg, wet, be,
                       rope_cos, rope_sin, decay, ident, identb, before, onesb, mean_mat, head_mean, one_rows,
                       expert_rank, expert_base, spare_slot, out):
    f32, bf16, u32 = mybir.dt.float32, mybir.dt.bfloat16, mybir.dt.uint32
    ALU, ACT, AX = mybir.AluOpType, mybir.ActivationFunctionType, mybir.AxisListType
    ds = bass.ds

    ctx = ExitStack()
    with ctx:
        def sb(name, shape, dt=f32):
            return ctx.enter_context(nc.sbuf_tensor(name, shape, dt))

        def sem(name):
            return ctx.enter_context(nc.semaphore(name))

        parts_dram = nc.dram_tensor("parts_dram", (2, 2, 3, 2 * HD, PAIRS, T), bf16, kind="Internal").ap()
        slots_in = nc.dram_tensor("slots_in", (2 * NTOK, D), f32, kind="Internal").ap()
        max_dram = [nc.dram_tensor(f"max_dram{i}", (4, PAIRS // 2, T), bf16, kind="Internal").ap() for i in range(2)]
        slots_out = nc.dram_tensor("slots_out", (NTOK, D), f32, kind="Internal").ap()

        wq_sb, wqr_sb = sb("wq_sb", [D, P]), sb("wqr_sb", [D, P])
        bq_sb, bqr_sb, bd_sb = sb("bq_sb", [P, 1]), sb("bqr_sb", [P, 1]), sb("bd_sb", [LAT, 1])
        wd_sb = sb("wd_sb", [D, LAT])
        wk_sb, wkr_sb, wv_sb = sb("wk_sb", [LAT + 1, P]), sb("wkr_sb", [LAT + 1, P]), sb("wv_sb", [LAT + 1, P])
        wo_sb, bo_sb, ones_row = sb("wo_sb", [P, D]), sb("bo_sb", [1, D]), sb("ones_row", [1, P])
        wg_sb, wet_sb, be_sb = sb("wg_sb", [D, NE]), sb("wet_sb", [D, NE * D]), sb("be_sb", [P, NE * D])
        cos_sb, sin_sb = sb("cos_sb", [P, T]), sb("sin_sb", [P, T])
        decay_sb = sb("decay_sb", [P, KT * T])
        id_sb, idb_sb = sb("id_sb", [P, P]), sb("idb_sb", [P, P], bf16)
        before_sb, onesb_sb = sb("before_sb", [P, P], bf16), sb("onesb_sb", [P, P], bf16)
        mean_sb, hmean_sb = sb("mean_sb", [P, P]), sb("hmean_sb", [P, NH])
        rank_sb, base_sb, spare_sb = sb("rank_sb", [P, NE]), sb("base_sb", [P, NE]), sb("spare_sb", [P, NT])

        x_all = sb("x_all", [P, NT, D])
        xn_all = sb("xn_all", [P, NT, D])
        xnT = sb("xnT", [D, NTOK])
        ffn_all = sb("ffn_all", [P, NT, D])
        xn_ring, xnT_ring = sb("xn_ring", [P, 2, CK, D]), sb("xnT_ring", [D, 2, CK * P])
        stats = sb("stats", [P, NT, 6])
        mean2, mgap, mgap2, msq, ssq, mean, var = (sb(n, [P, NT]) for n in ("mean2", "mgap", "mgap2", "msq", "ssq", "mean", "var"))
        std, rstd, eps_sb = sb("std", [P, NT]), sb("rstd", [P, NT]), sb("eps_sb", [P, 1])
        logits, hit, rank, mask = (sb(n, [P, NT, NE]) for n in ("logits", "hit", "rank", "mask"))
        maskb = sb("maskb", [P, NT, NE], bf16)
        shifted, expl = sb("shifted", [P, NT, NE]), sb("expl", [P, NT, NE])
        pre = [sb(f"pre{i}", [P, NT, NE]) for i in range(6)]
        where, picked, based = sb("where", [P, NT, NE]), sb("picked", [P, NT, NE]), sb("based", [P, NT, NE])
        top, toprank, denom, invden, gate = (sb(n, [P, NT]) for n in ("top", "toprank", "denom", "invden", "gate"))
        place, first, keep, slot, off, dest = (sb(n, [P, NT]) for n in ("place", "first", "keep", "slot", "off", "dest"))
        kept_slot, dest2 = sb("kept_slot", [P, NT]), sb("dest2", [P, NT])
        dest_u, src_u = sb("dest_u", [P, NT], u32), sb("src_u", [P, NT], u32)
        cT = [sb(f"cT{i}", [LAT + 1, T]) for i in range(2)]
        turn1, turn2 = sb("turn1", [P, 2, T]), sb("turn2", [P, 2, T])
        qk = [sb(f"qk{i}", [P, 2, T]) for i in range(2)]
        part = [sb(f"part{i}", [P, 2, T], bf16) for i in range(3)]
        rest = sb("rest", [P, 2, T])
        ksum = [sb(f"ksum{i}", [P, 1]) for i in range(2)]
        mk = [sb(f"mk{i}", [P, NH]) for i in range(2)]
        Qs = [sb(f"Qs{i}", [P, PAIRS, T], bf16) for i in range(2)]
        Ks = [sb(f"Ks{i}", [P, 2, PAIRS, T], bf16) for i in range(2)]
        Va = [sb(f"Va{i}", [P, KT, NH * 32]) for i in range(2)]
        negmax = [sb(f"negmax{i}", [P, KT, NH]) for i in range(2)]
        maxparts = sb("maxparts", [P, KT, 2, 16], bf16)
        maxT = [sb(f"maxT{i}", [16, T], bf16) for i in range(2)]
        probs = sb("probs", [P, NH, KT * T])
        Oacc = sb("Oacc", [P, 2, T])
        rden, Oq, OT = sb("rden", [P, 2 * NH]), sb("Oq", [P, 2 * NH, HD]), sb("OT", [P, T])
        Oraw = sb("Oraw", [P, 2 * NH, HD])
        th, gth = sb("th", [P, 2 * NH]), sb("gth", [P, 2 * NH])
        memo = [sb(f"memo{i}", [P, 2 * NH, HD]) for i in range(2)]
        exin, exT, exout = sb("exin", [P, CK, D]), sb("exT", [D, CK * P]), sb("exout", [P, CK, D])

        def bank(name):
            return ctx.enter_context(nc.psum_tensor(name, [P, 512], f32))

        Sb = [bank(f"scores{i}") for i in range(2)]
        Xb = [bank(f"raw{i}") for i in range(2)]
        PVb = bank("pv")
        Mb = [bank(f"misc{i}") for i in range(3)]

        w_early = sem("w_early")
        w_late = sem("w_late")
        zeroed = sem("zeroed")
        one_rows_in = sem("one_rows_in")
        init_dve = sem("init_dve")
        init_pool = sem("init_pool")
        stat = sem("stat")
        joined = sem("joined")
        var_done = sem("var_done")
        std_done = sem("std_done")
        rstd_done = sem("rstd_done")
        xn_done = sem("xn_done")
        xn_copied = sem("xn_copied")
        xT_done = sem("xT_done")
        xT_evac = sem("xT_evac")
        lg_done = sem("lg_done")
        lg_copied = sem("lg_copied")
        rt = sem("rt")
        rt_pe = sem("rt_pe")
        rt_exp = sem("rt_exp")
        rt_shift = sem("rt_shift")
        mask_done = sem("mask_done")
        routed = sem("routed")
        scattered = sem("scattered")
        c_done = sem("c_done")
        q_done = sem("q_done")
        mt_done = sem("mt_done")
        v_done = sem("v_done")
        k_done = sem("k_done")
        otr_done = sem("otr_done")
        mem_done = sem("mem_done")
        ft_done = sem("ft_done")
        o2t_done = sem("o2t_done")
        fo_done = sem("fo_done")
        wo_done = sem("wo_done")
        c_evac = sem("c_evac")
        q_rope = sem("q_rope")
        mt_evac = sem("mt_evac")
        v_evac = sem("v_evac")
        k_rope = sem("k_rope")
        o_raw = sem("o_raw")
        rden_done = sem("rden_done")
        th_done = sem("th_done")
        gth_done = sem("gth_done")
        memo_done = sem("memo_done")
        mk_done = sem("mk_done")
        o_ready = sem("o_ready")
        ft_evac = sem("ft_evac")
        o2t_evac = sem("o2t_evac")
        exout_done = sem("exout_done")
        y_done = sem("y_done")
        qk_done = sem("qk_done")
        rest_done = sem("rest_done")
        parts_out = sem("parts_out")
        raw_done = sem("raw_done")
        reduced = sem("reduced")
        maxhi = sem("maxhi")
        maxlo = sem("maxlo")
        s_done = sem("s_done")
        exp_done = sem("exp_done")
        mul_dve = sem("mul_dve")
        mul_pool = sem("mul_pool")
        pv_done = sem("pv_done")
        o_evac = sem("o_evac")
        ex_in = sem("ex_in")
        ex_stored = sem("ex_stored")
        gathered = sem("gathered")
        res_done = sem("res_done")
        out_done = sem("out_done")
        x_in = [sem(f"x_in{i}") for i in range(2)]
        mrow_in = [sem(f"mrow_in{i}") for i in range(2)]
        max_out = [sem(f"max_out{i}") for i in range(2)]
        stack_in = [[sem(f"stack_in{i}{j}") for j in range(2)] for i in range(2)]
        part_done = [sem(f"part_done{i}") for i in range(3)]
        block = ctx.enter_context(nc.Block())

        def count(n, most=None):
            if not isinstance(n, int):
                return n
            return max(0, n if most is None else min(n, most))

        def has(s):
            if not isinstance(s, int):
                return dict(proj=True, mx=True, attn=True, fin=True)
            return dict(proj=s + 1 < B, mx=0 <= s < B, attn=0 <= s - 1 < B, fin=0 <= s - 2 < B)

        def nothing():
            pass

        def run_steps(eng, step, after_first=nothing, after_second=nothing, after_loops=nothing):
            step(-1, 1, None, -1)
            after_first()
            step(0, 0, None, 0)
            after_second()
            step(1, 1, None, 0)
            step(2, 0, "on", 1)
            step(3, 1, "on", 1)
            for first, last, ffn in ((2, NCH // 2, "on"), (1 + NCH // 2, B // 2 - 2, "over")):
                with eng.Fori(first, last + 1) as u:
                    step(2 * u, 0, ffn, u)
                    step(2 * u + 1, 1, ffn, u)
            for s in range(B - 2, B + 2):
                if s == B - 1:
                    after_loops()
                step(s, s % 2, "over", s // 2)

        @block.sync
        def _(sp):
            sp.wait_ge(init_dve, 1)
            sp.dma_start(slots_in[0:NTOK, :].rearrange("(a p) d -> p a d", p=P), ffn_all[:, :, :]).then_inc(zeroed, 16)
            xv = x.rearrange("b (k p) d -> p (b k) d", p=P)
            for i in range(2):
                sp.dma_start(x_all[:, i * CK:(i + 1) * CK, :], xv[:, i * CK:(i + 1) * CK, :]).then_inc(x_in[i], 16)
            with sp.Fori(2, NCH - 1, 2) as c:
                for i in range(2):
                    t = sp.snap(c * CK + i * CK)
                    sp.wait_ge(x_in[i], count(c * 8))
                    sp.dma_start(x_all[:, ds(t, CK), :], xv[:, ds(t, CK), :]).then_inc(x_in[i], 16)

            def held(n):
                return n if isinstance(n, int) else sp.snap(sp.to_reg(n), min_val=1)

            def stack(p, par, half):
                done = stack_in[half][par]
                lo, n = half * PAIRS // 2, PAIRS // 2
                row = PAIRS * T
                for e in range(2):
                    at = HROWS * e
                    for (j, times), nk in zip(Q_STACK, K_STACK):
                        rows = times * HD
                        src = parts_dram[par, 0, j, HD * e:HD * (e + 1), lo:lo + n, :]
                        q_src = bass.AP(src.tensor, src.offset, [(0, times), (row, HD), (1, n * T)])
                        sp.dma_start(Qs[par][at:at + rows, lo:lo + n, :].rearrange("p g t -> p (g t)"),
                                     q_src).then_inc(done, 16)
                        src = parts_dram[par, 1, 0, HD * e:HD * (e + 1), lo:lo + n, :]
                        k_src = bass.AP(src.tensor, src.offset, [(2 * HD * row, nk), (row, HD), (1, n * T)])
                        sp.dma_start(Ks[par][at:at + rows, e, lo:lo + n, :].rearrange("p g t -> p (g t)"),
                                     k_src).then_inc(done, 16)
                        at += rows

            def max_rows(half, par, written):
                sp.dma_start(max_dram[half].rearrange("r g t -> (r g) t"), maxT[half][:, :]).then_inc(max_out[half], 16)
                sp.wait_ge(max_out[half], count(written))
                n = PAIRS // 2
                sp.dma_start(Qs[par][SROWS:SROWS + 4, n * half:n * half + n, :], max_dram[half]).then_inc(mrow_in[half], 16)

            def step(s, par, ffn, u):
                f = has(s)
                other = 1 - par
                c = s - 2
                at = {k: held(v) for k, v in (
                    ("s-1", s - 1), ("s-2", c), ("s+2", s + 2), ("2s", 2 * s), ("2s+1", 2 * s + 1), ("96s+192", 96 * s + 192), ("16s-8", 16 * s - 8), ("16s", 16 * s), ("16s+16", 16 * s + 16))}
                if ffn == "on":
                    first = held(c * (CK * P))
                    sp.wait_ge(scattered, 16 * NT)
                    sp.wait_ge(ft_done, count(at["s-2"]))
                    sp.dma_start(exin[:, :, :], slots_in[ds(first, CK * P), :].rearrange("(k p) d -> p k d", p=P)
                                 ).then_inc(ex_in, 16)
                if f["attn"]:
                    sp.wait_ge(mt_evac, count(at["2s"]))
                    max_rows(1, other, at["16s"])
                if f["proj"]:
                    p = s + 1
                    for i in range(3):
                        sp.wait_ge(part_done[i], count(at["s+2"]))
                        for t in range(2):
                            src = parts_dram[other, t, i, :, :, :]
                            to = bass.AP(src.tensor, src.offset, [(T, PAIRS), (PAIRS * T, 2 * HD), (1, T)])
                            sp.dma_start(to, part[i][:, t, :]).then_inc(parts_out, 16)
                    sp.wait_ge(parts_out, count(at["96s+192"]))
                    if f["attn"]:
                        sp.wait_ge(s_done, count(at["16s-8"]))
                    else:
                        sp.wait_ge(one_rows_in, 16)
                        sp.wait_ge(init_pool, 1)
                    stack(p, other, 0)
                if ffn == "on":
                    sp.wait_ge(exout_done, count(at["s-1"]))
                    sp.dma_start(slots_out[ds(first, CK * P), :].rearrange("(k p) d -> p k d", p=P), exout[:, :, :]
                                 ).then_inc(ex_stored, 16)
                if f["mx"]:
                    sp.wait_ge(mt_evac, count(at["2s+1"]))
                    max_rows(0, par, at["16s+16"])
                if f["proj"]:
                    if f["attn"]:
                        sp.wait_ge(s_done, count(at["16s"]))
                    stack(p, other, 1)

            run_steps(sp, step, nothing, nothing)
            ov = out.rearrange("b (k p) d -> p (b k) d", p=P)
            with sp.Fori(0, B) as b:
                sp.wait_ge(res_done, count(b + 1))
                sp.dma_start(ov[:, ds(b * KT, KT), :], x_all[:, ds(b * KT, KT), :]).then_inc(out_done, 16)
            sp.wait_ge(out_done, 16 * B)

        @block.gpsimd
        def _(pool):
            for i in range(2):
                nc.gpsimd.memset(Qs[i][:, :, :].rearrange("p g t -> p (g t)").bitcast(u32), 0)
                nc.gpsimd.memset(Va[i][:, :, :], 0.0)
                last = nc.gpsimd.memset(Ks[i][:, :, :, :].rearrange("p e g t -> p (e g t)").bitcast(u32), 0)
            last.then_inc(init_pool, 1)
            pool.wait_ge(init_pool, 1)
            for i in range(2):
                v = Va[i][:, :, :].rearrange("p k (g s r) -> p (k g) s r", s=2, r=32)
                nc.gpsimd.memset(v[:, :, 0, 8:9], 1.0)
                last = nc.gpsimd.memset(v[:, :, 1, 24:25], 1.0)
            last.then_inc(init_pool, 1)

            def step(s, par, ffn, u):
                f = has(s)
                other = 1 - par
                for i in range(NH):
                    if f["attn"] and i not in DVE_HEADS:
                        a, h = s - 1, HEADS[i]
                        pool.wait_ge(exp_done, count(16 * a + i + 1))
                        nc.gpsimd.tensor_tensor(probs[:, h, :], probs[:, h, :], decay_sb[:, :],
                                                op=ALU.mult).then_inc(mul_pool, 1)
                    if f["proj"] and i == 0:
                        p = s + 1
                        pool.wait_ge(q_rope, count(p + 1))
                        pool.wait_ge(k_rope, count(p + 1))
                        pool.wait_ge(mem_done, count(p - 1))
                        nc.gpsimd.tensor_tensor(qk[other][:, :, :], turn1[:, :, :], turn2[:, :, :],
                                                op=ALU.add).then_inc(qk_done, 1)
                    if f["proj"] and i == 2:
                        pool.wait_ge(part_done[0], count(p + 1))
                        pool.wait_ge(qk_done, count(p + 1))
                        nc.gpsimd.tensor_tensor(rest[:, :, :], qk[other][:, :, :], part[0][:, :, :],
                                                op=ALU.subtract).then_inc(rest_done, 1)
                    if f["proj"] and i == 5:
                        pool.wait_ge(part_done[1], count(p + 1))
                        pool.wait_ge(rest_done, count(p + 1))
                        pool.wait_ge(parts_out, count(96 * p))
                        nc.gpsimd.tensor_tensor(part[2][:, :, :], rest[:, :, :], part[1][:, :, :],
                                                op=ALU.subtract).then_inc(part_done[2], 1)
            def scatter():
                pool.wait_ge(routed, 1)
                pool.wait_ge(zeroed, 16)
                pool.wait_ge(xn_copied, NCH)
                for t in range(NT):
                    nc.gpsimd.indirect_dma_start(
                        out=slots_in[:, :], out_offset=bass.IndirectOffsetOnAxis(ap=dest_u[:, t:t + 1], axis=0),
                        in_=xn_all[:, t, :], in_offset=None).then_inc(scattered, 16)

            def gather():
                pool.wait_ge(ex_stored, 16 * NCH)
                for t in range(NT):
                    nc.gpsimd.indirect_dma_start(
                        out=ffn_all[:, t, :], out_offset=None, in_=slots_out[:, :],
                        in_offset=bass.IndirectOffsetOnAxis(ap=src_u[:, t:t + 1], axis=0)).then_inc(gathered, 16)

            run_steps(pool, step, nothing, scatter, gather)
            pool.wait_ge(gathered, 16 * NT)

        @block.scalar
        def _(act):
            for to, src in ((id_sb, ident), (wg_sb, wg)):
                act.dma_start(to[:, :], src).then_inc(w_early, 16)
            late = [(wq_sb, wq), (wqr_sb, wqr), (bq_sb, bq), (bqr_sb, bqr), (wd_sb, wd), (bd_sb, bd), (wk_sb, wk),
                    (wkr_sb, wkr), (wv_sb, wv), (cos_sb, rope_cos), (sin_sb, rope_sin), (idb_sb, identb),
                    (before_sb, before), (onesb_sb, onesb), (mean_sb, mean_mat), (hmean_sb, head_mean),
                    (rank_sb, expert_rank), (base_sb, expert_base), (spare_sb, spare_slot), (decay_sb, decay),
                    (wo_sb, wo), (bo_sb, bo), (wet_sb, wet), (be_sb, be.broadcast_to([P, NE * D]))]
            for to, src in late:
                act.dma_start(to[:, :], src).then_inc(w_late, 16)
            act.wait_ge(init_pool, 1)
            for i in range(2):
                for e in range(2):
                    act.dma_start(Ks[i][SROWS:SROWS + 4, e, :, :].rearrange("p g t -> p (g t)"),
                                  one_rows[e, :, :]).then_inc(one_rows_in, 16)
            act.wait_ge(init_dve, 2)
            act.wait_ge(var_done, 1)
            nc.scalar.activation(std[:, :], var[:, :], ACT.Sqrt, bias=eps_sb[:, 0:1]).then_inc(std_done, 1)

            def xT_out(c, i):
                act.wait_ge(xT_done, count(c + 1))
                nc.scalar.activation(xnT[:, ds(c * (CK * P), CK * P)], Sb[i][:, :], ACT.Identity)
                act.wait_ge(lg_done, count(c - 1))
                nc.scalar.activation(xnT_ring[:, i, :], Sb[i][:, :], ACT.Identity).then_inc(xT_evac, 1)

            xT_out(0, 0)
            xT_out(1, 1)
            with act.Fori(2, NCH - 1, 2) as c:
                xT_out(c, 0)
                xT_out(c + 1, 1)
            act.wait_ge(w_late, count(16 * len(late)))
            act.wait_ge(init_pool, 2)

            def step(s, par, ffn, u):
                f = has(s)
                other = 1 - par
                p, a, o = s + 1, s - 1, s - 2
                if f["proj"]:
                    act.wait_ge(c_done, count(p + 1))
                    nc.scalar.activation(cT[other][0:LAT, :], Mb[0][0:LAT, 0:T], ACT.Identity,
                                         bias=bd_sb[:, 0:1]).then_inc(c_evac, 1)
                if f["attn"]:
                    act.wait_ge(mt_done, count(2 * s))
                    act.wait_ge(mrow_in[1], count(16 * a))
                    nc.scalar.activation(maxT[1][:, :], Mb[2][0:16, 0:T // 2].bitcast(bf16),
                                         ACT.Identity).then_inc(mt_evac, 1)
                if f["fin"]:
                    act.wait_ge(pv_done, count(4 * o + 4))
                    nc.scalar.activation(Oacc[:, 1, :], PVb[:, T:2 * T], ACT.Identity).then_inc(o_evac, 1)
                if f["mx"]:
                    act.wait_ge(v_done, count(s + 1))
                    act.wait_ge(pv_done, count(4 * (s - 1)))
                    for k in range(KT):
                        to = Va[par][:, k, :].rearrange("p (g r) -> p g r", r=64)
                        src = Mb[0][:, k * P:(k + 1) * P].rearrange("p (g s d) -> p s g d", s=2, d=HD)
                        for e in range(2):
                            last = nc.scalar.activation(to[:, :, 48 * e:48 * e + HD], src[:, e, :, :], ACT.Identity)
                    last.then_inc(v_evac, 1)
                    act.wait_ge(mem_done, count(s + 1))
                    act.wait_ge(gth_done, count(s))
                    nc.scalar.activation(th[:, :], Mb[0][:, 0:2 * NH], ACT.Tanh, scale=0.5).then_inc(th_done, 1)

                def copy_slots():
                    act.wait_ge(ft_done, count(s - 1))
                    nc.scalar.activation(exT[:, :], Mb[1][:, :], ACT.Identity).then_inc(ft_evac, 1)

                def copy_o():
                    act.wait_ge(o2t_done, count(o + 1))
                    nc.scalar.activation(OT[:, :], Mb[2][:, 0:T], ACT.Identity).then_inc(o2t_evac, 1)

                if f["fin"] and not f["attn"]:
                    copy_o()
                for i in range(NH):
                    if f["attn"]:
                        h = HEADS[i]
                        act.wait_ge(s_done, count(16 * a + i + 1))
                        if i % 4 == 0:
                            act.wait_ge(pv_done, count(4 * (a - 1) + i // 4 + 1))
                        nc.scalar.activation(probs[:, h, :], Sb[i % 2][:, :], ACT.Exp,
                                             scale=SCALE).then_inc(exp_done, 1)
                    if ffn == "on" and i == 0:
                        copy_slots()
                    if f["fin"] and f["attn"] and i == 1:
                        copy_o()
                    if f["proj"] and i == 2:
                        act.wait_ge(qk_done, count(p + 1))
                        act.wait_ge(parts_out, count(96 * p))
                        nc.scalar.activation(part[0][:, 0, :], qk[other][:, 0, :], ACT.Identity)
                        act.wait_ge(mk_done, count(p - 1))
                        nc.scalar.activation(part[0][:, 1, :], qk[other][:, 1, :], ACT.Identity,
                                             accum_out=ksum[other][:, 0:1]).then_inc(part_done[0], 1)
                    if f["proj"] and i == 4:
                        act.wait_ge(rest_done, count(p + 1))
                        nc.scalar.activation(part[1][:, :, :], rest[:, :, :], ACT.Identity).then_inc(part_done[1], 1)
                    if f["mx"] and i == 11:
                        act.wait_ge(mt_done, count(2 * s + 1))
                        act.wait_ge(mrow_in[0], count(16 * s))
                        nc.scalar.activation(maxT[0][:, :], Mb[2][0:16, 0:T // 2].bitcast(bf16),
                                             ACT.Identity).then_inc(mt_evac, 1)
                    if f["attn"] and i == 12:
                        act.wait_ge(pv_done, count(4 * a + 2))
                        act.wait_ge(otr_done, count(a))
                        nc.scalar.activation(Oacc[:, 0, :], PVb[:, 0:T], ACT.Identity).then_inc(o_evac, 1)

            def gate_exp():
                act.wait_ge(rt_shift, 1)
                nc.scalar.activation(expl[:, :, :], shifted[:, :, :], ACT.Exp).then_inc(rt_exp, 1)

            run_steps(act, step, gate_exp, nothing)

        @block.vector
        def _(dve):
            nc.vector.memset(ffn_all[:, :, :], 0.0).then_inc(init_dve, 1)
            nc.vector.memset(ones_row[:, :], 1.0)
            for i in range(2):
                nc.vector.memset(cT[i][LAT:LAT + 1, :], 1.0)
            nc.vector.memset(eps_sb[:, :], LN_EPS).then_inc(init_dve, 1)

            def tile_stats(t):
                nc.vector.bn_stats(stats[:, ds(t, 1), :].rearrange("p a n -> p (a n)"),
                                   x_all[:, ds(t, 1), :].rearrange("p a n -> p (a n)")).then_inc(stat, 1)

            with dve.Fori(0, NCH - 1, 2) as c:
                for i in range(2):
                    dve.wait_ge(x_in[i], count(c * 8 + 16))
                    for k in range(CK):
                        tile_stats((c + i) * CK + k)
            dve.wait_ge(stat, NT)
            nc.vector.tensor_tensor(mean2[:, :], stats[:, :, 1], stats[:, :, 4], op=ALU.add)
            nc.vector.tensor_tensor(mgap[:, :], stats[:, :, 1], stats[:, :, 4], op=ALU.subtract)
            nc.vector.tensor_tensor(ssq[:, :], stats[:, :, 2], stats[:, :, 5], op=ALU.add).then_inc(joined, 1)
            dve.wait_ge(joined, 1)
            nc.vector.tensor_scalar(mean[:, :], mean2[:, :], 0.5, None, ALU.mult)
            nc.vector.tensor_scalar(mgap2[:, :], mgap[:, :], 0.5, None, ALU.mult).then_inc(joined, 1)
            dve.wait_ge(joined, 2)
            nc.vector.tensor_tensor(msq[:, :], mgap2[:, :], mgap2[:, :], op=ALU.mult).then_inc(joined, 1)
            dve.wait_ge(joined, 3)
            nc.vector.scalar_tensor_tensor(var[:, :], ssq[:, :], 1.0 / D, msq[:, :], op0=ALU.mult,
                                           op1=ALU.add).then_inc(var_done, 1)
            dve.wait_ge(std_done, 1)
            nc.vector.reciprocal(rstd[:, :], std[:, :]).then_inc(rstd_done, 1)
            dve.wait_ge(rstd_done, 1)

            def normalise(c, i):
                dve.wait_ge(xT_done, count(c - 1))
                dve.wait_ge(xn_copied, count(c - 1))
                for k in range(CK):
                    t = c * CK + k
                    last = nc.vector.tensor_scalar(
                        xn_ring[:, i, k, :], x_all[:, ds(t, 1), :].rearrange("p a n -> p (a n)"),
                        mean[:, ds(t, 1)], rstd[:, ds(t, 1)], ALU.subtract, ALU.mult)
                last.then_inc(xn_done, 1)

            def keep_normalised(c, i):
                dve.wait_ge(xn_done, count(c + 1))
                nc.vector.tensor_copy(xn_all[:, ds(c * CK, CK), :], xn_ring[:, i, :, :]).then_inc(xn_copied, 1)

            def logits_out(c, i):
                dve.wait_ge(lg_done, count(c + 1))
                nc.vector.tensor_copy(logits[:, ds(c * CK, CK), :].rearrange("p k e -> p (k e)"),
                                      Xb[i][:, 0:CK * NE]).then_inc(lg_copied, 1)

            normalise(0, 0)
            normalise(1, 1)
            keep_normalised(0, 0)
            keep_normalised(1, 1)
            with dve.Fori(2, NCH - 1, 2) as c:
                normalise(c, 0)
                normalise(c + 1, 1)
                keep_normalised(c, 0)
                keep_normalised(c + 1, 1)
                logits_out(c - 2, 0)
                logits_out(c - 1, 1)
            logits_out(NCH - 2, 0)
            logits_out(NCH - 1, 1)

            def step(s, par, ffn, u):
                f = has(s)
                other = 1 - par
                p, a, o = s + 1, s - 1, s - 2
                if f["proj"]:
                    dve.wait_ge(q_done, count(p + 1))
                    dve.wait_ge(qk_done, count(p))
                    nc.vector.scalar_tensor_tensor(turn1[:, 0, :], Mb[1][:, 0:T], bq_sb[:, 0:1], cos_sb[:, :],
                                                   op0=ALU.add, op1=ALU.mult)
                    nc.vector.scalar_tensor_tensor(turn2[:, 0, :], Mb[1][:, T:2 * T], bqr_sb[:, 0:1], sin_sb[:, :],
                                                   op0=ALU.add, op1=ALU.mult).then_inc(q_rope, 1)
                    dve.wait_ge(k_done, count(p + 1))
                    nc.vector.tensor_tensor(turn1[:, 1, :], Mb[1][:, 0:T], cos_sb[:, :], op=ALU.mult)
                    nc.vector.tensor_tensor(turn2[:, 1, :], Mb[1][:, T:2 * T], sin_sb[:, :],
                                            op=ALU.mult).then_inc(k_rope, 1)
                if f["mx"]:
                    dve.wait_ge(part_done[0], count(s + 1))
                    dve.wait_ge(mem_done, count(s - 1))
                    nc.vector.tensor_scalar(mk[par][:, :], hmean_sb[:, :], ksum[par][:, 0:1], None,
                                            ALU.mult).then_inc(mk_done, 1)
                if f["fin"]:
                    dve.wait_ge(otr_done, count(o + 1))
                    dve.wait_ge(o_ready, count(o))
                    otr = Mb[2][:, :].rearrange("p (h r) -> p h r", r=2 * HD)
                    nc.vector.reciprocal(rden[:, :], otr[:, :, HD]).then_inc(rden_done, 1)
                    dve.wait_ge(rden_done, count(o + 1))
                    nc.vector.tensor_tensor(Oraw[:, :, :], otr[:, :, 0:HD],
                                            rden[:, :].unsqueeze(2).broadcast_to([P, 2 * NH, HD]),
                                            op=ALU.mult).then_inc(o_raw, 1)
                    dve.wait_ge(o_raw, count(o + 1))
                    dve.wait_ge(memo_done, count(o + 1))
                    dve.wait_ge(o2t_done, count(o))
                    nc.vector.tensor_tensor(Oq[:, :, :], Oraw[:, :, :], memo[par][:, :, :],
                                            op=ALU.add).then_inc(o_ready, 1)
                if f["mx"]:
                    dve.wait_ge(th_done, count(s + 1))
                    dve.wait_ge(memo_done, count(s))
                    nc.vector.tensor_scalar(gth[:, :], th[:, :], 0.1, 0.1, ALU.mult, ALU.add).then_inc(gth_done, 1)
                    dve.wait_ge(gth_done, count(s + 1))
                    dve.wait_ge(o_ready, count(s - 1))
                    nc.vector.tensor_tensor(
                        memo[par][:, :, :].rearrange("p (k h) d -> p k h d", k=KT),
                        Mb[0][:, P:2 * P].rearrange("p (k h d) -> p k h d", k=1, d=HD).broadcast_to([P, KT, NH, HD]),
                        gth[:, :].rearrange("p (k h d) -> p k h d", k=KT, d=1).broadcast_to([P, KT, NH, HD]),
                        op=ALU.mult).then_inc(memo_done, 1)

                def experts_out():
                    c = s - 2
                    dve.wait_ge(fo_done, count(c + 1))
                    dve.wait_ge(ex_stored, count(16 * c))
                    nc.vector.tensor_tensor(
                        exout[:, :, :], Mb[0][:, :].rearrange("p (k d) -> p k d", d=D),
                        be_sb[:, ds(c * D, D)].rearrange("p (k d) -> p k d", k=1).broadcast_to([P, CK, D]),
                        op=ALU.add).then_inc(exout_done, 1)

                def residual():
                    dve.wait_ge(wo_done, count(o + 1))
                    xa = x_all[:, ds(o * KT, KT), :].rearrange("p k d -> p (k d)")
                    nc.vector.tensor_tensor(xa, Mb[1][:, 0:KT * D], xa, op=ALU.add).then_inc(y_done, 1)

                def split_max(half):
                    n = 8 * half + 8
                    src = negmax[par][:, :, 8 * half:8 * half + 8].rearrange("p k (g e) -> p k g e", e=2)
                    to = maxparts[:, :, half, :].rearrange("p k (e l g) -> p k l g e", e=2, l=2)
                    dve.wait_ge(reduced, count(16 * s + n))
                    dve.wait_ge(mt_done, count(2 * s + half - 1))
                    nc.vector.tensor_copy(to[:, :, 0, :, :], src).then_inc(maxhi, 1)
                    dve.wait_ge(maxhi, count(2 * s + half + 1))
                    nc.vector.tensor_tensor(to[:, :, 1, :, :], src, to[:, :, 0, :, :],
                                            op=ALU.subtract).then_inc(maxlo, 1)

                if f["fin"] and not f["attn"]:
                    residual()
                for i in range(NH):
                    if f["mx"]:
                        g, qt = i // 2, i % 2
                        dve.wait_ge(raw_done, count(16 * s + i + 1))
                        nc.vector.tensor_reduce(negmax[par][:, qt, 2 * g:2 * g + 2],
                                                Xb[i % 2][:, :].rearrange("p (h k) -> p h k", h=2),
                                                axis=AX.X, op=ALU.max, negate=True).then_inc(reduced, 1)
                        if i == 8:
                            split_max(0)
                    if f["attn"] and i - 1 in DVE_HEADS:
                        h = HEADS[i - 1]
                        dve.wait_ge(exp_done, count(16 * a + i))
                        nc.vector.tensor_tensor(probs[:, h, :], probs[:, h, :], decay_sb[:, :],
                                                op=ALU.mult).then_inc(mul_dve, 1)
                    if ffn == "on" and i == 3:
                        experts_out()
                    if f["fin"] and f["attn"] and i == 5:
                        residual()
                if f["attn"] and NH - 1 in DVE_HEADS:
                    h = HEADS[NH - 1]
                    dve.wait_ge(exp_done, count(16 * a + NH))
                    nc.vector.tensor_tensor(probs[:, h, :], probs[:, h, :], decay_sb[:, :],
                                            op=ALU.mult).then_inc(mul_dve, 1)
                if f["mx"]:
                    split_max(1)

            def route():
                seq = [0]

                def then(ins):
                    seq[0] += 1
                    ins.then_inc(rt, 1)
                    dve.wait_ge(rt, seq[0])

                def wide(v):
                    return v[:, :].unsqueeze(2).broadcast_to([P, NT, NE])

                def each(v):
                    return v[:, :].unsqueeze(1).broadcast_to([P, NT, NE])

                dve.wait_ge(w_late, 16 * 24)
                dve.wait_ge(lg_copied, NCH)
                then(nc.vector.tensor_reduce(top[:, :], logits[:, :, :], axis=AX.X, op=ALU.max))
                nc.vector.tensor_tensor(shifted[:, :, :], logits[:, :, :], wide(top), op=ALU.subtract).then_inc(rt_shift, 1)
                then(nc.vector.tensor_tensor(hit[:, :, :], logits[:, :, :], wide(top), op=ALU.is_equal))
                then(nc.vector.tensor_tensor(rank[:, :, :], hit[:, :, :], each(rank_sb), op=ALU.mult))
                then(nc.vector.tensor_reduce(toprank[:, :], rank[:, :, :], axis=AX.X, op=ALU.max))
                then(nc.vector.tensor_tensor(mask[:, :, :], rank[:, :, :], wide(toprank), op=ALU.is_equal))
                nc.vector.tensor_copy(maskb[:, :, :], mask[:, :, :]).then_inc(mask_done, 1)
                dve.wait_ge(rt_pe, 2)
                then(nc.vector.tensor_copy(pre[0][:, :, :], Xb[1][:, 0:NT * NE].rearrange("p (t e) -> p t e", e=NE)))
                for i in range(5):
                    d = 1 << i
                    nc.vector.tensor_copy(pre[i + 1][:, 0:d, :], pre[i][:, 0:d, :])
                    then(nc.vector.tensor_tensor(pre[i + 1][:, d:NT, :], pre[i][:, d:NT, :], pre[i][:, 0:NT - d, :], op=ALU.add))
                v = Xb[0][:, 0:NT * NE].rearrange("p (t e) -> p t e", e=NE)
                nc.vector.tensor_copy(where[:, 0:1, :], v[:, 0:1, :])
                then(nc.vector.tensor_tensor(where[:, 1:NT, :], v[:, 1:NT, :], pre[5][:, 0:NT - 1, :], op=ALU.add))
                then(nc.vector.tensor_tensor(picked[:, :, :], where[:, :, :], mask[:, :, :], op=ALU.mult))
                then(nc.vector.tensor_reduce(place[:, :], picked[:, :, :], axis=AX.X, op=ALU.add))
                then(nc.vector.tensor_tensor(based[:, :, :], mask[:, :, :], each(base_sb), op=ALU.mult))
                then(nc.vector.tensor_reduce(first[:, :], based[:, :, :], axis=AX.X, op=ALU.add))
                then(nc.vector.tensor_scalar(keep[:, :], place[:, :], float(CAP), None, ALU.is_lt))
                then(nc.vector.tensor_tensor(slot[:, :], first[:, :], place[:, :], op=ALU.add))
                then(nc.vector.tensor_tensor(kept_slot[:, :], slot[:, :], keep[:, :], op=ALU.mult))
                nc.vector.tensor_copy(src_u[:, :], kept_slot[:, :])
                then(nc.vector.tensor_tensor(off[:, :], slot[:, :], spare_sb[:, :], op=ALU.subtract))
                then(nc.vector.tensor_tensor(dest[:, :], off[:, :], keep[:, :], op=ALU.mult))
                then(nc.vector.tensor_tensor(dest2[:, :], dest[:, :], spare_sb[:, :], op=ALU.add))
                nc.vector.tensor_copy(dest_u[:, :], dest2[:, :]).then_inc(routed, 1)
                dve.wait_ge(rt_exp, 1)
                then(nc.vector.tensor_reduce(denom[:, :], expl[:, :, :], axis=AX.X, op=ALU.add))
                then(nc.vector.reciprocal(invden[:, :], denom[:, :]))
                then(nc.vector.tensor_tensor(gate[:, :], invden[:, :], keep[:, :], op=ALU.mult))

            run_steps(dve, step, route, nothing)
            dve.wait_ge(gathered, 16 * NT)
            dve.wait_ge(y_done, B)
            with dve.Fori(0, B) as b:
                for k in range(KT):
                    t = b * KT + k
                    xa = x_all[:, ds(t, 1), :].rearrange("p a n -> p (a n)")
                    last = nc.vector.scalar_tensor_tensor(xa, ffn_all[:, ds(t, 1), :].rearrange("p a n -> p (a n)"),
                                                          gate[:, ds(t, 1)], xa, op0=ALU.mult, op1=ALU.add)
                last.then_inc(res_done, 1)

        @block.tensor
        def _(pe):
            pe.wait_ge(w_early, 32)

            def turn_tokens(c, i):
                pe.wait_ge(xn_done, count(c + 1))
                pe.wait_ge(xT_evac, count(c - 1))
                for k in range(CK):
                    last = nc.tensor.transpose(Sb[i][:, k * P:(k + 1) * P], xn_ring[:, i, k, :], id_sb[:, :])
                last.then_inc(xT_done, 1)

            def router(c, i):
                pe.wait_ge(xT_evac, count(c + 1))
                pe.wait_ge(lg_copied, count(c - 1))
                for k in range(CK):
                    last = nc.tensor.matmul(Xb[i][:, k * NE:(k + 1) * NE], xnT_ring[:, i, k * P:(k + 1) * P], wg_sb[:, :],
                                            start=True, stop=True)
                last.then_inc(lg_done, 1)

            turn_tokens(0, 0)
            turn_tokens(1, 1)
            router(0, 0)
            turn_tokens(2, 0)
            router(1, 1)
            turn_tokens(3, 1)
            with pe.Fori(4, NCH - 1, 2) as c:
                router(c - 2, 0)
                turn_tokens(c, 0)
                router(c - 1, 1)
                turn_tokens(c + 1, 1)
            router(NCH - 2, 0)
            router(NCH - 1, 1)
            pe.wait_ge(w_late, 16 * 24)
            pe.wait_ge(init_dve, 2)
            pe.wait_ge(init_pool, 2)
            pe.wait_ge(one_rows_in, 64)

            def step(s, par, ffn, u):
                f = has(s)
                other = 1 - par
                p, a, o = s + 1, s - 1, s - 2

                experts_before = count(s - 2, NCH) if ffn != "over" else NCH
                experts_now = count(s - 1, NCH) if ffn != "over" else NCH

                def pv(b, slot, g):
                    heads = HEADS[4 * g:4 * g + 4]
                    half, e = g // 2, g % 2
                    done = [i for i in range(NH) if i < 4 * g + 4]
                    pe.wait_ge(mul_pool, count(b * (NH - len(DVE_HEADS)) + sum(i not in DVE_HEADS for i in done)))
                    pe.wait_ge(mul_dve, count(b * len(DVE_HEADS) + sum(i in DVE_HEADS for i in done)))
                    if e == 0:
                        pe.wait_ge(o_evac, count(2 * b + half))
                    for k in range(KT):
                        for j, h in enumerate(heads):
                            last = nc.tensor.matmul(PVb[32 * j:32 * j + 32, half * T:(half + 1) * T],
                                                    Va[slot][:, k, 32 * h:32 * h + 32],
                                                    probs[:, h, k * T:(k + 1) * T],
                                                    start=(e == 0 and k == 0), stop=(e == 1 and k == KT - 1))
                    last.then_inc(pv_done, 1)

                if f["proj"]:
                    xb = xnT[:, ds(p * T, T)]
                    pe.wait_ge(memo_done, count(s, B))
                    pe.wait_ge(exout_done, experts_before)
                    m = Mb[0]
                    nc.tensor.matmul(m[0:LAT, 0:T], wd_sb[:, :], xb, start=True, stop=True).then_inc(c_done, 1)
                    pe.wait_ge(k_rope, count(s + 1, B))
                    pe.wait_ge(y_done, count(s - 2, B))
                    m = Mb[1]
                    nc.tensor.matmul(m[:, 0:T], wq_sb[:, :], xb, start=True, stop=True)
                    nc.tensor.matmul(m[:, T:2 * T], wqr_sb[:, :], xb, start=True, stop=True).then_inc(q_done, 1)
                if f["attn"]:
                    pe.wait_ge(mt_evac, count(2 * s - 1, 2 * B))
                    pe.wait_ge(o2t_evac, count(s - 2, B))
                    m = Mb[2]
                    pe.wait_ge(maxlo, count(2 * s))
                    for k in range(KT):
                        last = nc.tensor.transpose(m[0:16, k * P // 2:(k + 1) * P // 2].bitcast(bf16),
                                                   maxparts[:, k, 1, :], idb_sb[:, :])
                    last.then_inc(mt_done, 1)
                if f["fin"]:
                    pv(o, par, 3)
                if f["mx"]:
                    pe.wait_ge(c_evac, count(s + 2, B))
                    pe.wait_ge(memo_done, count(s, B))
                    pe.wait_ge(exout_done, experts_before)
                    m = Mb[0]
                    pe.wait_ge(c_evac, count(s + 1))
                    for k in range(KT):
                        last = nc.tensor.matmul(m[:, k * P:(k + 1) * P], cT[par][:, k * P:(k + 1) * P], wv_sb[:, :],
                                                start=True, stop=True)
                    last.then_inc(v_done, 1)
                if f["proj"]:
                    pe.wait_ge(q_rope, count(s + 2, B))
                    m = Mb[1]
                    pe.wait_ge(c_evac, count(p + 1))
                    nc.tensor.matmul(m[:, 0:T], wk_sb[:, :], cT[other][:, :], start=True, stop=True)
                    nc.tensor.matmul(m[:, T:2 * T], wkr_sb[:, :], cT[other][:, :], start=True,
                                     stop=True).then_inc(k_done, 1)
                if f["fin"]:
                    pe.wait_ge(mt_evac, count(2 * s, 2 * B))
                    pe.wait_ge(o2t_evac, count(s - 2, B))
                    m = Mb[2]
                    pe.wait_ge(o_evac, count(2 * o + 2))
                    for q in range(KT):
                        for half in range(2):
                            at = (2 * q + half) * P
                            last = nc.tensor.transpose(m[:, at:at + P], Oacc[:, half, q * P:(q + 1) * P], id_sb[:, :])
                    last.then_inc(otr_done, 1)
                if f["mx"]:
                    pe.wait_ge(v_evac, count(s + 1, B))
                    m = Mb[0]
                    pe.wait_ge(mk_done, count(s + 1))
                    for k in range(KT):
                        nc.tensor.matmul(m[:, k * NH:(k + 1) * NH], qk[par][:, 0, k * P:(k + 1) * P], mk[par][:, :],
                                         start=True, stop=True)
                    pe.wait_ge(v_evac, count(s + 1))
                    for k in range(KT):
                        v = Va[par][:, k, :].rearrange("p (g r) -> p g r", r=64)
                        for e in range(2):
                            to = m[:, P:2 * P].rearrange("p (g e d) -> p e g d", e=2, d=HD)[:, e]
                            last = nc.tensor.matmul(to, mean_sb[:, :], v[:, :, 48 * e:48 * e + HD],
                                                    start=(k == 0 and e == 0), stop=(k == KT - 1),
                                                    skip_group_check=True)
                    last.then_inc(mem_done, 1)

                def o2t():
                    pe.wait_ge(o_raw, count(o + 1))
                    m = Mb[2]
                    pe.wait_ge(o_ready, count(o + 1))
                    for k in range(KT):
                        last = nc.tensor.transpose(m[:, k * P:(k + 1) * P],
                                                   Oq[:, k * NH:(k + 1) * NH, :].rearrange("p h d -> p (h d)"), id_sb[:, :])
                    last.then_inc(o2t_done, 1)

                def out_proj():
                    pe.wait_ge(k_rope, count(s + 2, B))
                    pe.wait_ge(ft_evac, experts_now)
                    m = Mb[1]
                    pe.wait_ge(o2t_evac, count(o + 1))
                    for k in range(KT):
                        nc.tensor.matmul(m[:, k * D:(k + 1) * D], ones_row[:, :], bo_sb[:, :], start=True, stop=False)
                        last = nc.tensor.matmul(m[:, k * D:(k + 1) * D], OT[:, k * P:(k + 1) * P], wo_sb[:, :],
                                                start=False, stop=True)
                    last.then_inc(wo_done, 1)

                if f["fin"] and not f["attn"]:
                    o2t()
                    out_proj()
                for i in range(NH):
                    if f["attn"]:
                        h = HEADS[i]
                        g, e = h // 2, h % 2
                        if i % 8 == 0:
                            pe.wait_ge(mrow_in[i // 8], count(16 * (a + 1)))
                        pe.wait_ge(exp_done, count(16 * a + i - 1))
                        for k in range(KT):
                            last = nc.tensor.matmul(Sb[i % 2][:, k * T:(k + 1) * T],
                                                    Ks[other][:, e, g, k * P:(k + 1) * P], Qs[other][:, g, :],
                                                    start=True, stop=True)
                        last.then_inc(s_done, 1)
                    if f["mx"]:
                        g, q = i // 2, i % 2
                        if i % 8 == 0:
                            pe.wait_ge(stack_in[i // 8][par], count(192 * (u + 1)))
                        pe.wait_ge(reduced, count(16 * s + i - 1))
                        nc.tensor.matmul(Xb[i % 2][:, :], Qs[par][0:SROWS, g, q * P:(q + 1) * P],
                                         Ks[par][0:SROWS, :, g, :], start=True, stop=True).then_inc(raw_done, 1)
                    if ffn == "on" and i == 0:
                        pe.wait_ge(k_rope, count(s + 2, B))
                        m = Mb[1]
                        pe.wait_ge(ex_in, count(16 * (s - 1)))
                        for k in range(CK):
                            last = nc.tensor.transpose(m[:, k * P:(k + 1) * P], exin[:, k, :], id_sb[:, :])
                        last.then_inc(ft_done, 1)
                    if f["fin"] and f["attn"] and i == 1:
                        o2t()
                    if ffn == "on" and i == 2:
                        pe.wait_ge(memo_done, count(s + 1, B))
                        m = Mb[0]
                        pe.wait_ge(ft_evac, count(s - 1))
                        for k in range(CK):
                            last = nc.tensor.matmul(m[:, k * D:(k + 1) * D], exT[:, k * P:(k + 1) * P],
                                                    wet_sb[:, ds((s - 2) * D, D)], start=True, stop=True)
                        last.then_inc(fo_done, 1)
                    if f["fin"] and f["attn"] and i == 3:
                        out_proj()
                    if f["attn"] and i in (6, 10, 14):
                        pv(a, other, (i - 6) // 4)
                    if f["mx"] and i == 10:
                        pe.wait_ge(mt_evac, count(2 * s, 2 * B))
                        pe.wait_ge(o2t_evac, count(s - 1, B))
                        m = Mb[2]
                        pe.wait_ge(maxlo, count(2 * s + 1))
                        for k in range(KT):
                            last = nc.tensor.transpose(m[0:16, k * P // 2:(k + 1) * P // 2].bitcast(bf16),
                                                       maxparts[:, k, 0, :], idb_sb[:, :])
                        last.then_inc(mt_done, 1)

            def count_tokens():
                pe.wait_ge(mask_done, 1)
                pe.wait_ge(lg_copied, NCH)
                mb = maskb[:, :, :].rearrange("p t e -> p (t e)")
                nc.tensor.matmul(Xb[0][:, 0:NT * NE], before_sb[:, :], mb, start=True, stop=True).then_inc(rt_pe, 1)
                nc.tensor.matmul(Xb[1][:, 0:NT * NE], onesb_sb[:, :], mb, start=True, stop=True).then_inc(rt_pe, 1)

            run_steps(pe, step, count_tokens, nothing)


def _tables():
    bf = np.dtype("bfloat16")
    f = np.float32
    inv = (f(1.0) / np.power(f(10000.0), np.arange(0, HD, 2, dtype=f) / f(HD))).astype(f)
    freq = np.outer(np.arange(T, dtype=f), inv).astype(f)
    cos, sin = np.cos(freq).astype(f).T, np.sin(freq).astype(f).T
    rope_cos = np.tile(np.concatenate([cos, cos]), (NH, 1))
    rope_sin = np.tile(np.concatenate([-sin, sin]), (NH, 1))
    i = np.arange(T, dtype=np.float64)
    d = i[None, :] - i[:, None]
    dec = np.exp(-0.1 * np.log(np.abs(d) + 1.0)) * (np.exp(-np.maximum(d, 0.0) * 0.01) + 1e-9)
    decay = dec.reshape(KT, P, T).transpose(1, 0, 2).reshape(P, KT * T)
    ident = np.eye(P)
    before = np.triu(np.ones((P, P)), 1)
    head_mean = np.repeat(np.eye(NH), HD, axis=0) / T
    one_rows = np.zeros((2, 4, PAIRS * T))
    for e in range(2):
        one_rows[e, 2 * e:2 * e + 2] = 1.0
    rank = np.tile(np.arange(NE, 0, -1.0), (P, 1))
    base = np.tile(np.arange(NE) * float(CAP), (P, 1))
    spare = NTOK + np.arange(NTOK, dtype=f).reshape(NT, P).T
    c = np.ascontiguousarray
    return [c(rope_cos, f), c(rope_sin, f), c(decay, f), c(ident, f), c(ident).astype(bf), before.astype(bf),
            np.ones((P, P)).astype(bf), np.full((P, P), 1.0 / T, f), c(head_mean, f), one_rows.astype(bf),
            c(rank, f), c(base, f), c(spare, f)]


def kernel(**inputs):
    import concourse.bacc as _bacc
    from concourse import mybir as _mybir
    from concourse.bass_utils import run_bass_kernel_spmd as _run

    a = {k.replace("L0_", ""): np.asarray(v) for k, v in inputs.items()}
    swap = (np.arange(NH * HD).reshape(NH, 2, HD // 2)[:, ::-1]).reshape(-1)
    up = np.concatenate([a["attn_Wkv_up"], a["attn_bkv_up"][None, :]])
    up = up.reshape(LAT + 1, NH, 2, HD)
    wk, wv = up[:, :, 0].reshape(LAT + 1, P), up[:, :, 1].reshape(LAT + 1, P)
    wet = a["ffn_W"].transpose(2, 0, 1).reshape(D, NE * D)
    arrs = [a["attn_x"], a["attn_Wq"], a["attn_Wq"][:, swap], a["attn_bq"][:, None], a["attn_bq"][swap][:, None],
            a["attn_Wkv_down"], a["attn_bkv_down"][:, None], wk, wk[:, swap], wv, a["attn_Wo"], a["attn_bo"][None, :],
            a["ffn_wg"], wet, a["ffn_b"].reshape(1, NE * D)] + _tables()
    names = ["x", "wq", "wqr", "bq", "bqr", "wd", "bd", "wk", "wkr", "wv", "wo", "bo", "wg", "wet", "be",
             "rope_cos", "rope_sin", "decay", "ident", "identb", "before", "onesb", "mean_mat", "head_mean", "one_rows",
             "expert_rank", "expert_base", "spare_slot"]
    nc = _bacc.Bacc("TRN2", target_bir_lowering=False, num_devices=1)
    arrays, args = {}, []
    for name, v in zip(names, arrs):
        v = np.ascontiguousarray(v)
        arrays[f"in_{name}_dram"] = v
        args.append(nc.dram_tensor(f"in_{name}_dram", v.shape, _mybir.dt.from_np(v.dtype), kind="ExternalInput").ap())
    args.append(nc.dram_tensor("out_0_dram", (B, T, D), _mybir.dt.float32, kind="ExternalOutput").ap())
    mixed_block_kernel(nc, *args)
    r = _run(nc, [arrays], core_ids=[0])
    return r.results[0]["out_0_dram"]
```

```python
import numpy as np
import concourse.bass as bass
from concourse import mybir
from contextlib import ExitStack

B, T, D = 16, 256, 128
NH, HD = 16, 8
LAT = 32
NE = 8
P = 128
KT = T // P
NT = B * KT
NTOK = B * T
CAP = NTOK // NE
CK = 4
NCH = NT // CK
GROUP = NH // 2
Q_STACK = ((0, 3), (1, 2), (2, 1))
K_STACK = 3, 2, 1
MROW = 96
HEADS = [0, 2, 4, 6, 1, 3, 5, 7, 8, 10, 12, 14, 9, 11, 13, 15]
DVE_HEADS = (2, 6, 9, 11)
PE_HEADS = (4, 12)
X_LOADS = 0, CK, 2 * CK, 5 * CK, NT
FFN_AFTER = 3
SCATTERS = {0: (0, 14), 1: (14, 22), 2: (22, NT)}
GATHERS = {12: (0, 6), 13: (6, 12), 14: (12, 18), 15: (18, 24), 16: (24, NT)}
MORE_PE_HEADS = (1, 5, 8, 13)
SLOTS = 18
SCORES = (0, 1, 1, 2, 3, 4, 5, 6, 7, 8, 9, 10, 11, 12, 13, 14)
RAW_FROM = 1
DVE_SLOT = (4, 8, 10, 13)
PV_SLOT = (7, 11, 15)
PE = dict(max2=2, ex_in=6, pv2=4, o_turn=5, mem=6, o_back=8, ex_out=9, values=12, wo=11, max1=12, cq=14, k=16)
EV = dict(max2=2, part1=1, part2=5, ex_in=7, pv2=4, mem=7, o_back=9, values=12, max1=12, pv1=13, cq=14)
VE = dict(means=4, o_turn=6, mem=7, ex_out=10, max1=10, wo=12, cq=14, k=17)
POOL_QK, POOL_REST, POOL_PART3 = 0, 2, 5
SCALE = float(1.0 / np.sqrt(np.float32(HD)))
LN_EPS = 1e-5


def mixed_block_kernel(nc, x, wq, wqr, bq, bqr, wd, bd, wk, wkr, wv, wo, bo, wg, wet, be,
                       rope_cos, rope_sin, decay, log_decay, ident, identb, before, onesb, head_mean, one_rows,
                       expert_rank, expert_base, spare_slot, out):
    f32, bf16, u32 = mybir.dt.float32, mybir.dt.bfloat16, mybir.dt.uint32
    ALU, ACT, AX = mybir.AluOpType, mybir.ActivationFunctionType, mybir.AxisListType
    ds = bass.ds

    ctx = ExitStack()
    with ctx:
        def sb(name, shape, dt=f32):
            return ctx.enter_context(nc.sbuf_tensor(name, shape, dt))

        def sem(name):
            return ctx.enter_context(nc.semaphore(name))

        parts_dram = nc.dram_tensor("parts_dram", (2, 3, 2, P, T), bf16, kind="Internal").ap()
        slots_in = nc.dram_tensor("slots_in", (2 * NTOK, D), f32, kind="Internal").ap()
        max_dram = [nc.dram_tensor(f"max_dram{i}", (2, GROUP, T), bf16, kind="Internal").ap() for i in range(2)]
        slots_out = nc.dram_tensor("slots_out", (NTOK, D), f32, kind="Internal").ap()

        wq_sb, wqr_sb = sb("wq_sb", [D, P]), sb("wqr_sb", [D, P])
        bq_sb, bqr_sb, bd_sb = sb("bq_sb", [P, 1]), sb("bqr_sb", [P, 1]), sb("bd_sb", [LAT, 1])
        wd_sb = sb("wd_sb", [D, LAT])
        wk_sb, wkr_sb, wv_sb = sb("wk_sb", [LAT + 1, P]), sb("wkr_sb", [LAT + 1, P]), sb("wv_sb", [LAT + 1, P])
        wo_sb, bo_sb = sb("wo_sb", [P, D]), sb("bo_sb", [P, D])
        wg_sb, wet_sb, be_sb = sb("wg_sb", [D, NE]), sb("wet_sb", [D, NE * D]), sb("be_sb", [P, NE * D])
        cos_sb, sin_sb = sb("cos_sb", [P, T]), sb("sin_sb", [P, T])
        decay_sb, logd_sb = sb("decay_sb", [P, KT * T]), sb("logd_sb", [P, 3 * KT * T], bf16)
        id_sb, idb_sb = sb("id_sb", [P, P]), sb("idb_sb", [P, P], bf16)
        before_sb, onesb_sb = sb("before_sb", [P, P], bf16), sb("onesb_sb", [P, P], bf16)
        hmean_sb = sb("hmean_sb", [P, NH])
        rank_sb, base_sb, spare_sb = sb("rank_sb", [P, NE]), sb("base_sb", [P, NE]), sb("spare_sb", [P, NT])

        x_all = sb("x_all", [P, NT, D])
        xn_all = sb("xn_all", [P, NT, D])
        xnT = sb("xnT", [D, NTOK])
        ffn_all = sb("ffn_all", [P, NT, D])
        stats = sb("stats", [P, NT, 6])
        mean2, mgap, mgap2, msq, ssq, mean, var = (sb(n, [P, NT]) for n in ("mean2", "mgap", "mgap2", "msq", "ssq", "mean", "var"))
        std, rstd, eps_sb = sb("std", [P, NT]), sb("rstd", [P, NT]), sb("eps_sb", [P, 1])
        logits, hit, rank, mask = (sb(n, [P, NT, NE]) for n in ("logits", "hit", "rank", "mask"))
        maskb = sb("maskb", [P, NT, NE], bf16)
        shifted, expl = sb("shifted", [P, NT, NE]), sb("expl", [P, NT, NE])
        pre = [sb(f"pre{i}", [P, NT, NE]) for i in range(6)]
        where, picked, based = sb("where", [P, NT, NE]), sb("picked", [P, NT, NE]), sb("based", [P, NT, NE])
        top, toprank, denom, invden, gate = (sb(n, [P, NT]) for n in ("top", "toprank", "denom", "invden", "gate"))
        place, first, keep, slot, off, dest = (sb(n, [P, NT]) for n in ("place", "first", "keep", "slot", "off", "dest"))
        kept_slot, dest2 = sb("kept_slot", [P, NT]), sb("dest2", [P, NT])
        dest_u, src_u = sb("dest_u", [P, NT], u32), sb("src_u", [P, NT], u32)
        cT = [sb(f"cT{i}", [LAT + 1, T]) for i in range(2)]
        turn1, turn2 = sb("turn1", [P, 2, T]), sb("turn2", [P, 2, T])
        qk = [sb(f"qk{i}", [P, 2, T]) for i in range(2)]
        part = [sb(f"part{i}", [P, 2, T], bf16) for i in range(3)]
        rest = sb("rest", [P, 2, T])
        ksum = [sb(f"ksum{i}", [P, 1]) for i in range(2)]
        mk = [sb(f"mk{i}", [P, NH]) for i in range(2)]
        csum = [sb(f"csum{i}", [LAT, 1]) for i in range(2)]
        cmean = [sb(f"cmean{i}", [LAT + 1, P]) for i in range(2)]
        ones_lat = sb("ones_lat", [LAT, P])
        Qs = [[sb(f"Qs{i}_{e}", [P, GROUP, T], bf16) for e in range(2)] for i in range(2)]
        Ks = [[sb(f"Ks{i}_{e}", [P, GROUP, T], bf16) for e in range(2)] for i in range(2)]
        Va = [sb(f"Va{i}", [P, KT, NH * 32]) for i in range(2)]
        negmax = [sb(f"negmax{i}", [P, KT, NH]) for i in range(2)]
        maxparts = sb("maxparts", [P, KT, 2, 16], bf16)
        maxT = [sb(f"maxT{i}", [16, T], bf16) for i in range(2)]
        probs = sb("probs", [P, NH, KT * T])
        xn_ring = probs[:, 0:2, :].rearrange("p i (k d) -> p i k d", d=D)
        xnT_ring = probs[:, 2:4, :]
        Oacc = sb("Oacc", [P, 2, T])
        rden, Oq, OT = sb("rden", [P, 2 * NH]), sb("Oq", [P, 2 * NH, HD]), sb("OT", [P, T])
        Oraw = sb("Oraw", [P, 2 * NH, HD])
        th, gth = sb("th", [P, 2 * NH]), sb("gth", [P, 2 * NH])
        memo = [sb(f"memo{i}", [P, 2 * NH, HD]) for i in range(2)]
        exin, exT, exout = sb("exin", [P, CK, D]), sb("exT", [D, CK * P]), sb("exout", [P, CK, D])

        def bank(name):
            return ctx.enter_context(nc.psum_tensor(name, [P, 512], f32))

        Sb = [bank(f"scores{i}") for i in range(2)]
        Xb = [bank(f"raw{i}") for i in range(2)]
        PVb = bank("pv")
        Mb = [bank(f"misc{i}") for i in range(3)]

        w_early = sem("w_early")
        w_late = sem("w_late")
        biased = sem("biased")
        zeroed = sem("zeroed")
        one_rows_in = sem("one_rows_in")
        init_dve = sem("init_dve")
        init_pool = sem("init_pool")
        init_ffn = sem("init_ffn")
        stat = sem("stat")
        joined = sem("joined")
        var_done = sem("var_done")
        std_done = sem("std_done")
        rstd_done = sem("rstd_done")
        xn_done = sem("xn_done")
        xn_copied = sem("xn_copied")
        xT_done = sem("xT_done")
        xT_evac = sem("xT_evac")
        lg_done = sem("lg_done")
        lg_copied = sem("lg_copied")
        rt = sem("rt")
        rt_pe = sem("rt_pe")
        rt_exp = sem("rt_exp")
        rt_shift = sem("rt_shift")
        mask_done = sem("mask_done")
        routed = sem("routed")
        scattered = sem("scattered")
        c_done = sem("c_done")
        q_done = sem("q_done")
        mt_done = sem("mt_done")
        v_done = sem("v_done")
        k_done = sem("k_done")
        otr_done = sem("otr_done")
        mem_done = sem("mem_done")
        ft_done = sem("ft_done")
        o2t_done = sem("o2t_done")
        fo_done = sem("fo_done")
        wo_done = sem("wo_done")
        c_evac = sem("c_evac")
        q_rope = sem("q_rope")
        mt_evac = sem("mt_evac")
        v_evac = sem("v_evac")
        k_rope = sem("k_rope")
        o_raw = sem("o_raw")
        rden_done = sem("rden_done")
        th_done = sem("th_done")
        gth_done = sem("gth_done")
        memo_done = sem("memo_done")
        mk_done = sem("mk_done")
        cmean_done = sem("cmean_done")
        o_ready = sem("o_ready")
        ft_evac = sem("ft_evac")
        o2t_evac = sem("o2t_evac")
        exout_done = sem("exout_done")
        y_done = sem("y_done")
        qk_done = sem("qk_done")
        rest_done = sem("rest_done")
        parts_out = sem("parts_out")
        raw_done = sem("raw_done")
        reduced = sem("reduced")
        maxhi = sem("maxhi")
        maxlo = sem("maxlo")
        s_done = sem("s_done")
        exp_done = sem("exp_done")
        mul_dve = sem("mul_dve")
        mul_pool = sem("mul_pool")
        pv_done = sem("pv_done")
        o_evac = sem("o_evac")
        ex_in = sem("ex_in")
        ex_stored = sem("ex_stored")
        gathered = [sem(f"gathered{i}") for i in range(len(GATHERS))]
        res_done = sem("res_done")
        out_done = sem("out_done")
        x_in = [sem(f"x_in{i}") for i in range(len(X_LOADS) - 1)]
        mrow_in = [sem(f"mrow_in{i}") for i in range(2)]
        max_out = [sem(f"max_out{i}") for i in range(2)]
        stack_in = [[sem(f"stack_in{i}_{e}") for e in range(2)] for i in range(2)]
        part_done = [sem(f"part_done{i}") for i in range(3)]
        block = ctx.enter_context(nc.Block())

        FINISHED = {s + 1: (first // KT, last // KT) for s, (first, last) in GATHERS.items() if last < NT}
        BATCHES_LAST = max(last for _, last in FINISHED.values())

        def log_heads(b):
            return PE_HEADS + (MORE_PE_HEADS if isinstance(b, int) and not 2 <= b < 2 + NCH else ())

        def pool_heads(b):
            return [i for i in range(NH) if i not in DVE_HEADS + log_heads(b)]

        def pool_mults(b, places):
            if isinstance(b, int):
                before = sum(len(pool_heads(j)) for j in range(b))
            else:
                before = (b - 2) * len(pool_heads(b)) + sum(len(pool_heads(j)) for j in range(2))
            return before + sum(i < places for i in pool_heads(b))

        def count(n, most=None):
            if not isinstance(n, int):
                return n
            return max(0, n if most is None else min(n, most))

        def values_of(i, k):
            v = Va[i][:, k, :]
            return bass.AP(v.tensor, v.offset, [v.ap[0], (64, GROUP), (48, 2), (1, HD)])

        def has(s):
            if not isinstance(s, int):
                return dict(pre=True, proj=True, mx=True, attn=True, fin=True)
            return dict(pre=s + 2 < B, proj=-1 <= s < B - 1, mx=0 <= s < B, attn=0 <= s - 1 < B, fin=0 <= s - 2 < B)

        def run_steps(eng, step, from_step=0):
            if from_step == 0:
                step(0, 0, None, 0)
            step(1, 1, None, 0)
            step(2, 0, None, 1)
            step(3, 1, "on", 1)
            with eng.Fori(2, (NCH + FFN_AFTER - 1) // 2) as u:
                step(2 * u, 0, "on", u)
                step(2 * u + 1, 1, "on", u)
            for s in range(NCH + FFN_AFTER - 1, B + 2):
                step(s, s % 2, "on" if s < NCH + FFN_AFTER else "over", s // 2)

        @block.sync
        def _(sp):
            xv = x.rearrange("b (k p) d -> p (b k) d", p=P)
            for i, (first, last) in enumerate(zip(X_LOADS, X_LOADS[1:])):
                sp.dma_start(x_all[:, first:last, :], xv[:, first:last, :]).then_inc(x_in[i], 16)
            sp.wait_ge(init_ffn, 1)
            sp.dma_start(slots_in[0:NTOK, :].rearrange("(a p) d -> p a d", p=P), ffn_all[:, :, :]).then_inc(zeroed, 16)

            def held(n):
                return n if isinstance(n, int) else sp.snap(sp.to_reg(n), min_val=1)

            def stack(par, e, j):
                row = GROUP * T
                one_part = 2 * P * T
                times, nk = Q_STACK[j][1], K_STACK[j]
                at = HD * sum(t for _, t in Q_STACK[:j])
                rows = times * HD
                src = parts_dram[par, j, 0, e * P // 2:(e + 1) * P // 2, :]
                q_src = bass.AP(src.tensor, src.offset, [(0, times), (row, HD), (1, row)])
                sp.dma_start(Qs[par][e][at:at + rows, :, :].rearrange("p g t -> p (g t)"),
                             q_src).then_inc(stack_in[par][e], 16)
                src = parts_dram[par, 0, 1, e * P // 2:(e + 1) * P // 2, :]
                k_src = bass.AP(src.tensor, src.offset, [(one_part, nk), (row, HD), (1, row)])
                sp.dma_start(Ks[par][e][at:at + rows, :, :].rearrange("p g t -> p (g t)"),
                             k_src).then_inc(stack_in[par][e], 16)

            def max_rows_out(half):
                sp.dma_start(max_dram[half].rearrange("r g t -> (r g) t"), maxT[half][:, :]).then_inc(max_out[half], 16)

            def max_rows_in(half, par):
                sp.dma_start(Qs[par][half][MROW:MROW + 2, :, :], max_dram[half]).then_inc(mrow_in[half], 16)

            ov = out.rearrange("b (k p) d -> p (b k) d", p=P)

            def outputs(first, last):
                with sp.Fori(first, last) as b:
                    sp.wait_ge(res_done, count(b + 1))
                    sp.dma_start(ov[:, ds(b * KT, KT), :], x_all[:, ds(b * KT, KT), :]).then_inc(out_done, 16)

            def step(s, par, ffn, u):
                f = has(s)
                other = 1 - par
                c = s - FFN_AFTER
                at = {k: held(v) for k, v in (
                    ("c", c), ("c+1", c + 1), ("s+2", s + 2), ("2s", 2 * s), ("2s+1", 2 * s + 1), ("48s+96", 48 * s + 96), ("16s", 16 * s), ("16s-8", 16 * s - 8), ("16s+16", 16 * s + 16))}
                if ffn == "on":
                    first = held(c * (CK * P))
                    sp.wait_ge(scattered, 16 * NT)
                    sp.wait_ge(ft_done, count(at["c"]))
                    sp.dma_start(exin[:, :, :], slots_in[ds(first, CK * P), :].rearrange("(k p) d -> p k d", p=P)
                                 ).then_inc(ex_in, 16)
                if f["attn"]:
                    sp.wait_ge(mt_evac, count(at["2s"]))
                    max_rows_out(1)
                if f["proj"]:
                    sp.wait_ge(part_done[0], count(at["s+2"]))
                    sp.dma_start(parts_dram[other, 0].rearrange("t p n -> p t n"), part[0][:, :, :]).then_inc(parts_out, 16)
                if f["attn"]:
                    sp.wait_ge(max_out[1], count(at["16s"]))
                    max_rows_in(1, other)
                if f["proj"]:
                    for i in (1, 2):
                        sp.wait_ge(part_done[i], count(at["s+2"]))
                        sp.dma_start(parts_dram[other, i].rearrange("t p n -> p t n"), part[i][:, :, :]).then_inc(parts_out, 16)
                    sp.wait_ge(parts_out, count(at["48s+96"]))
                    if f["attn"]:
                        sp.wait_ge(s_done, count(at["16s-8"]))
                    else:
                        sp.wait_ge(init_pool, 1)
                    stack(other, 0, 0)
                    stack(other, 0, 1)
                    stack(other, 0, 2)
                if f["mx"]:
                    sp.wait_ge(mt_evac, count(at["2s+1"]))
                    max_rows_out(0)
                    sp.wait_ge(max_out[0], count(at["16s+16"]))
                    max_rows_in(0, par)
                if f["proj"]:
                    if f["attn"]:
                        sp.wait_ge(s_done, count(at["16s"]))
                    stack(other, 1, 0)
                    stack(other, 1, 1)
                    stack(other, 1, 2)
                if ffn == "on":
                    sp.wait_ge(exout_done, count(at["c+1"]))
                    sp.dma_start(slots_out[ds(first, CK * P), :].rearrange("(k p) d -> p k d", p=P), exout[:, :, :]
                                 ).then_inc(ex_stored, 16)
                if ffn == "over" and s - 1 in FINISHED:
                    outputs(*FINISHED[s - 1])

            step(-2, 0, None, -1)
            step(-1, 1, None, -1)
            run_steps(sp, step)
            outputs(BATCHES_LAST, B)
            sp.wait_ge(out_done, 16 * B)

        @block.gpsimd
        def _(pool):
            for i in range(2):
                nc.gpsimd.memset(Va[i][:, :, :], 0.0)
                for half in range(2):
                    nc.gpsimd.memset(Qs[i][half][:, :, :].rearrange("p g t -> p (g t)").bitcast(u32), 0)
                    last = nc.gpsimd.memset(Ks[i][half][:, :, :].rearrange("p g t -> p (g t)").bitcast(u32), 0)
            last.then_inc(init_pool, 1)
            pool.wait_ge(init_pool, 1)
            nc.gpsimd.memset(ffn_all[:, :, :], 0.0).then_inc(init_ffn, 1)
            for i in range(2):
                v = Va[i][:, :, :].rearrange("p k (g s r) -> p (k g) s r", s=2, r=32)
                nc.gpsimd.memset(v[:, :, 0, 8:9], 1.0)
                last = nc.gpsimd.memset(v[:, :, 1, 24:25], 1.0)
            last.then_inc(init_pool, 1)

            def scatter(t):
                nc.gpsimd.indirect_dma_start(
                    out=slots_in[:, :], out_offset=bass.IndirectOffsetOnAxis(ap=dest_u[:, t:t + 1], axis=0),
                    in_=xn_all[:, t, :], in_offset=None).then_inc(scattered, 16)

            def gather(t, done):
                nc.gpsimd.indirect_dma_start(
                    out=ffn_all[:, t, :], out_offset=None, in_=slots_out[:, :],
                    in_offset=bass.IndirectOffsetOnAxis(ap=src_u[:, t:t + 1], axis=0)).then_inc(done, 16)

            def step(s, par, ffn, u):
                f = has(s)
                other = 1 - par
                first, last = (0, 0) if ffn == "on" or s < 1 else SCATTERS.get(s) or GATHERS.get(s) or (0, 0)
                if ffn == "over" and s in GATHERS:
                    pool.wait_ge(ex_stored, 16 * NCH)
                for i in range(NH):
                    if first + i < last and ffn is None:
                        scatter(first + i)
                    if first + i < last and ffn == "over":
                        gather(first + i, gathered[list(GATHERS).index(s)])
                    if f["proj"] and i == POOL_QK:
                        p = s + 1
                        pool.wait_ge(q_rope, count(p + 1))
                        pool.wait_ge(k_rope, count(p + 1))
                        pool.wait_ge(mem_done, count(p - 1))
                        nc.gpsimd.tensor_tensor(qk[other][:, :, :], turn1[:, :, :], turn2[:, :, :],
                                                op=ALU.add).then_inc(qk_done, 1)
                    if f["attn"] and i in pool_heads(s - 1):
                        a, h = s - 1, HEADS[i]
                        pool.wait_ge(exp_done, count(16 * a + i + 1))
                        nc.gpsimd.tensor_tensor(probs[:, h, :], probs[:, h, :], decay_sb[:, :],
                                                op=ALU.mult).then_inc(mul_pool, 1)
                    if f["proj"] and i == POOL_REST:
                        pool.wait_ge(part_done[0], count(p + 1))
                        pool.wait_ge(qk_done, count(p + 1))
                        nc.gpsimd.tensor_tensor(rest[:, :, :], qk[other][:, :, :], part[0][:, :, :],
                                                op=ALU.subtract).then_inc(rest_done, 1)
                    if f["proj"] and i == POOL_PART3:
                        pool.wait_ge(part_done[1], count(p + 1))
                        pool.wait_ge(rest_done, count(p + 1))
                        pool.wait_ge(parts_out, count(48 * p))
                        nc.gpsimd.tensor_tensor(part[2][:, :, :], rest[:, :, :], part[1][:, :, :],
                                                op=ALU.subtract).then_inc(part_done[2], 1)

            step(-2, 0, None, -1)
            step(-1, 1, None, -1)
            pool.wait_ge(xn_done, NCH)
            pool.wait_ge(w_late, 16 * 24)
            nc.gpsimd.tensor_tensor(x_all[:, :, :], x_all[:, :, :], bo_sb[:, :].unsqueeze(1).broadcast_to([P, NT, D]),
                                    op=ALU.add).then_inc(biased, 1)
            step(0, 0, None, 0)
            pool.wait_ge(routed, 1)
            pool.wait_ge(zeroed, 16)
            pool.wait_ge(xn_copied, NCH)
            for t in range(*SCATTERS[0]):
                scatter(t)
            run_steps(pool, step, from_step=1)
            for i, (first, last) in enumerate(GATHERS.values()):
                pool.wait_ge(gathered[i], 16 * (last - first))

        @block.scalar
        def _(act):
            for to, src in ((id_sb, ident), (wg_sb, wg)):
                act.dma_start(to[:, :], src).then_inc(w_early, 16)
            late = [(wq_sb, wq), (wqr_sb, wqr), (bq_sb, bq), (bqr_sb, bqr), (wd_sb, wd), (bd_sb, bd), (wk_sb, wk),
                    (wkr_sb, wkr), (wv_sb, wv), (cos_sb, rope_cos), (sin_sb, rope_sin), (idb_sb, identb),
                    (before_sb, before), (onesb_sb, onesb), (hmean_sb, head_mean),
                    (rank_sb, expert_rank), (base_sb, expert_base), (spare_sb, spare_slot), (decay_sb, decay), (logd_sb, log_decay),
                    (wo_sb, wo), (bo_sb, bo.broadcast_to([P, D])), (wet_sb, wet), (be_sb, be.broadcast_to([P, NE * D]))]
            for to, src in late:
                act.dma_start(to[:, :], src).then_inc(w_late, 16)
            act.wait_ge(init_pool, 1)
            for i in range(2):
                for e in range(2):
                    act.dma_start(Ks[i][e][MROW:MROW + 2, :, :].rearrange("p g t -> p (g t)"), one_rows).then_inc(one_rows_in, 16)
            act.wait_ge(init_dve, 1)
            act.wait_ge(var_done, 1)
            nc.scalar.activation(std[:, :], var[:, :], ACT.Sqrt, bias=eps_sb[:, 0:1]).then_inc(std_done, 1)

            def xT_out(c, i):
                act.wait_ge(xT_done, count(c + 1))
                nc.scalar.activation(xnT[:, ds(c * (CK * P), CK * P)], Sb[i][:, :], ACT.Identity)
                act.wait_ge(lg_done, count(c - 1))
                nc.scalar.activation(xnT_ring[:, i, :], Sb[i][:, :], ACT.Identity).then_inc(xT_evac, 1)


            def step(s, par, ffn, u):
                f = has(s)
                other = 1 - par
                p, a, o = s + 1, s - 1, s - 2
                for t in range(SLOTS):
                    if f["attn"]:
                        for i in [i for i in range(NH) if SCORES[i] == t]:
                            h = HEADS[i]
                            act.wait_ge(s_done, count(16 * a + i + 1))
                            if i % 4 == 0:
                                act.wait_ge(pv_done, count(4 * (a - 1) + i // 4 + 1))
                            nc.scalar.activation(probs[:, h, :], Sb[i % 2][:, :], ACT.Exp,
                                                 scale=SCALE).then_inc(exp_done, 1)
                    if f["attn"] and t == EV["max2"]:
                        act.wait_ge(mt_done, count(2 * s))
                        act.wait_ge(mrow_in[1], count(16 * a))
                        nc.scalar.activation(maxT[1][:, :], Mb[2][0:16, 0:T // 2].bitcast(bf16),
                                             ACT.Identity).then_inc(mt_evac, 1)
                    if f["proj"] and t == EV["part1"]:
                        act.wait_ge(qk_done, count(p + 1))
                        act.wait_ge(parts_out, count(48 * p))
                        nc.scalar.activation(part[0][:, 0, :], qk[other][:, 0, :], ACT.Identity)
                        act.wait_ge(mk_done, count(p - 1))
                        nc.scalar.activation(part[0][:, 1, :], qk[other][:, 1, :], ACT.Identity,
                                             accum_out=ksum[other][:, 0:1]).then_inc(part_done[0], 1)
                    if ffn == "on" and t == EV["ex_in"]:
                        act.wait_ge(ft_done, s - FFN_AFTER + 1)
                        nc.scalar.activation(exT[:, :], Mb[1][:, :], ACT.Identity).then_inc(ft_evac, 1)
                    if f["fin"] and t == EV["pv2"]:
                        act.wait_ge(pv_done, count(4 * o + 4))
                        nc.scalar.activation(Oacc[:, 1, :], PVb[:, T:2 * T], ACT.Identity).then_inc(o_evac, 1)
                    if f["proj"] and t == EV["part2"]:
                        act.wait_ge(rest_done, count(p + 1))
                        nc.scalar.activation(part[1][:, :, :], rest[:, :, :], ACT.Identity).then_inc(part_done[1], 1)
                    if f["mx"] and t == EV["mem"]:
                        act.wait_ge(mem_done, count(s + 1))
                        act.wait_ge(gth_done, count(s))
                        nc.scalar.activation(th[:, :], Mb[0][:, 0:2 * NH], ACT.Tanh, scale=0.5).then_inc(th_done, 1)
                    if f["fin"] and t == EV["o_back"]:
                        act.wait_ge(o2t_done, count(o + 1))
                        nc.scalar.activation(OT[:, :], Mb[2][:, 0:T], ACT.Identity).then_inc(o2t_evac, 1)
                    if f["mx"] and t == EV["values"]:
                        act.wait_ge(v_done, count(s + 1))
                        act.wait_ge(pv_done, count(4 * (s - 1)))
                        for k in range(KT):
                            last = nc.scalar.activation(values_of(par, k),
                                                        Mb[0][:, k * P:(k + 1) * P].rearrange("p (g e d) -> p g e d", e=2, d=HD),
                                                        ACT.Identity)
                        last.then_inc(v_evac, 1)
                    if f["mx"] and t == EV["max1"]:
                        act.wait_ge(mt_done, count(2 * s + 1))
                        act.wait_ge(mrow_in[0], count(16 * s))
                        nc.scalar.activation(maxT[0][:, :], Mb[2][0:16, 0:T // 2].bitcast(bf16),
                                             ACT.Identity).then_inc(mt_evac, 1)
                    if f["pre"] and t == EV["cq"]:
                        act.wait_ge(c_done, count(s + 3))
                        act.wait_ge(cmean_done, count(s + 1))
                        nc.scalar.activation(cT[par][0:LAT, :], Mb[0][0:LAT, 0:T], ACT.Identity,
                                             bias=bd_sb[:, 0:1], accum_out=csum[par][:, 0:1]).then_inc(c_evac, 1)
                    if f["attn"] and t == EV["pv1"]:
                        act.wait_ge(pv_done, count(4 * a + 2))
                        act.wait_ge(otr_done, count(a))
                        nc.scalar.activation(Oacc[:, 0, :], PVb[:, 0:T], ACT.Identity).then_inc(o_evac, 1)

            def gate_exp():
                act.wait_ge(rt_shift, 1)
                nc.scalar.activation(expl[:, :, :], shifted[:, :, :], ACT.Exp).then_inc(rt_exp, 1)

            xT_out(0, 0)
            xT_out(1, 1)
            act.wait_ge(w_late, count(16 * len(late)))
            act.wait_ge(init_pool, 2)
            step(-2, 0, None, -1)
            xT_out(2, 0)
            xT_out(3, 1)
            step(-1, 1, None, -1)
            with act.Fori(4, NCH - 1, 2) as c:
                xT_out(c, 0)
                xT_out(c + 1, 1)
            gate_exp()
            run_steps(act, step)

        @block.vector
        def _(dve):
            for i in range(2):
                nc.vector.memset(cT[i][LAT:LAT + 1, :], 1.0)
                nc.vector.memset(cmean[i][LAT:LAT + 1, :], 1.0)
            nc.vector.memset(ones_lat[:, :], 1.0)
            nc.vector.memset(eps_sb[:, :], LN_EPS).then_inc(init_dve, 1)

            def tile_stats(t):
                nc.vector.bn_stats(stats[:, ds(t, 1), :].rearrange("p a n -> p (a n)"),
                                   x_all[:, ds(t, 1), :].rearrange("p a n -> p (a n)")).then_inc(stat, 1)

            for i in range(len(x_in)):
                dve.wait_ge(x_in[i], 16)
                with dve.Fori(X_LOADS[i], X_LOADS[i + 1] - CK + 1, CK) as t:
                    for k in range(CK):
                        tile_stats(t + k)
            dve.wait_ge(stat, NT)
            nc.vector.tensor_tensor(mean2[:, :], stats[:, :, 1], stats[:, :, 4], op=ALU.add)
            nc.vector.tensor_tensor(mgap[:, :], stats[:, :, 1], stats[:, :, 4], op=ALU.subtract)
            nc.vector.tensor_tensor(ssq[:, :], stats[:, :, 2], stats[:, :, 5], op=ALU.add).then_inc(joined, 1)
            dve.wait_ge(joined, 1)
            nc.vector.tensor_scalar(mean[:, :], mean2[:, :], 0.5, None, ALU.mult)
            nc.vector.tensor_scalar(mgap2[:, :], mgap[:, :], 0.5, None, ALU.mult).then_inc(joined, 1)
            dve.wait_ge(joined, 2)
            nc.vector.tensor_tensor(msq[:, :], mgap2[:, :], mgap2[:, :], op=ALU.mult).then_inc(joined, 1)
            dve.wait_ge(joined, 3)
            nc.vector.scalar_tensor_tensor(var[:, :], ssq[:, :], 1.0 / D, msq[:, :], op0=ALU.mult,
                                           op1=ALU.add).then_inc(var_done, 1)
            dve.wait_ge(std_done, 1)
            nc.vector.reciprocal(rstd[:, :], std[:, :]).then_inc(rstd_done, 1)
            dve.wait_ge(rstd_done, 1)

            def normalise(c, i):
                dve.wait_ge(xT_done, count(c - 1))
                dve.wait_ge(xn_copied, count(c - 1))
                for k in range(CK):
                    t = c * CK + k
                    last = nc.vector.tensor_scalar(
                        xn_ring[:, i, k, :], x_all[:, ds(t, 1), :].rearrange("p a n -> p (a n)"),
                        mean[:, ds(t, 1)], rstd[:, ds(t, 1)], ALU.subtract, ALU.mult)
                last.then_inc(xn_done, 1)

            def keep_normalised(c, i):
                dve.wait_ge(xn_done, count(c + 1))
                nc.vector.tensor_copy(xn_all[:, ds(c * CK, CK), :], xn_ring[:, i, :, :]).then_inc(xn_copied, 1)

            def logits_out(c, i):
                dve.wait_ge(lg_done, count(c + 1))
                nc.vector.tensor_copy(logits[:, ds(c * CK, CK), :].rearrange("p k e -> p (k e)"),
                                      Xb[i][:, 0:CK * NE]).then_inc(lg_copied, 1)

            def step(s, par, ffn, u):
                f = has(s)
                other = 1 - par
                p, a, o = s + 1, s - 1, s - 2

                def split_max(half):
                    n = 8 * half + 8
                    src = negmax[par][:, :, 8 * half:8 * half + 8]
                    to = maxparts[:, :, half, :].rearrange("p k (l g) -> p k l g", l=2)
                    dve.wait_ge(reduced, count(16 * s + n))
                    dve.wait_ge(mt_done, count(2 * s + half - 1))
                    nc.vector.tensor_copy(to[:, :, 0, :], src).then_inc(maxhi, 1)
                    dve.wait_ge(maxhi, count(2 * s + half + 1))
                    nc.vector.tensor_tensor(to[:, :, 1, :], src, to[:, :, 0, :],
                                            op=ALU.subtract).then_inc(maxlo, 1)

                for t in range(SLOTS):
                    i = t - RAW_FROM
                    if f["mx"] and 0 <= i < 16:
                        g, qt = i // 2, i % 2
                        dve.wait_ge(raw_done, count(16 * s + i + 1))
                        nc.vector.tensor_reduce(negmax[par][:, qt, 2 * g:2 * g + 2],
                                                Xb[i % 2][:, :].rearrange("p (h k) -> p h k", h=2),
                                                axis=AX.X, op=ALU.max, negate=True).then_inc(reduced, 1)
                    if f["mx"] and t == VE["means"]:
                        dve.wait_ge(part_done[0], count(s + 1))
                        dve.wait_ge(c_evac, count(s + 1))
                        dve.wait_ge(mem_done, count(s - 1))
                        nc.vector.tensor_scalar(mk[par][:, :], hmean_sb[:, :], ksum[par][:, 0:1], None,
                                                ALU.mult).then_inc(mk_done, 1)
                        nc.vector.tensor_scalar(cmean[par][0:LAT, :], ones_lat[:, :], csum[par][:, 0:1], 1.0 / T,
                                                ALU.mult, ALU.mult).then_inc(cmean_done, 1)
                    if f["fin"] and t == VE["o_turn"]:
                        dve.wait_ge(otr_done, count(o + 1))
                        dve.wait_ge(o_ready, count(o))
                        otr = Mb[2][:, :].rearrange("p (h r) -> p h r", r=2 * HD)
                        nc.vector.reciprocal(rden[:, :], otr[:, :, HD]).then_inc(rden_done, 1)
                        dve.wait_ge(rden_done, count(o + 1))
                        nc.vector.tensor_tensor(Oraw[:, :, :], otr[:, :, 0:HD],
                                                rden[:, :].unsqueeze(2).broadcast_to([P, 2 * NH, HD]),
                                                op=ALU.mult).then_inc(o_raw, 1)
                        dve.wait_ge(o_raw, count(o + 1))
                        dve.wait_ge(memo_done, count(o + 1))
                        dve.wait_ge(o2t_done, count(o))
                        nc.vector.tensor_tensor(Oq[:, :, :], Oraw[:, :, :], memo[par][:, :, :],
                                                op=ALU.add).then_inc(o_ready, 1)
                    if f["mx"] and t == VE["mem"]:
                        dve.wait_ge(th_done, count(s + 1))
                        dve.wait_ge(memo_done, count(s))
                        nc.vector.tensor_scalar(gth[:, :], th[:, :], 0.1, 0.1, ALU.mult, ALU.add).then_inc(gth_done, 1)
                        dve.wait_ge(gth_done, count(s + 1))
                        dve.wait_ge(o_ready, count(s - 1))
                        nc.vector.tensor_tensor(
                            memo[par][:, :, :].rearrange("p (k h) d -> p k h d", k=KT),
                            Mb[0][:, P:2 * P].rearrange("p (k h d) -> p k h d", k=1, d=HD).broadcast_to([P, KT, NH, HD]),
                            gth[:, :].rearrange("p (k h d) -> p k h d", k=KT, d=1).broadcast_to([P, KT, NH, HD]),
                            op=ALU.mult).then_inc(memo_done, 1)
                    if f["attn"] and t in DVE_SLOT:
                        i = DVE_HEADS[DVE_SLOT.index(t)]
                        h = HEADS[i]
                        dve.wait_ge(exp_done, count(16 * a + i + 1))
                        nc.vector.tensor_tensor(probs[:, h, :], probs[:, h, :], decay_sb[:, :],
                                                op=ALU.mult).then_inc(mul_dve, 1)
                    if ffn == "on" and t == VE["ex_out"]:
                        c = s - FFN_AFTER
                        dve.wait_ge(fo_done, count(c + 1))
                        dve.wait_ge(ex_stored, count(16 * c))
                        nc.vector.tensor_tensor(
                            exout[:, :, :], Mb[0][:, :].rearrange("p (k d) -> p k d", d=D),
                            be_sb[:, ds(c * D, D)].rearrange("p (k d) -> p k d", k=1).broadcast_to([P, CK, D]),
                            op=ALU.add).then_inc(exout_done, 1)
                    if f["mx"] and t == VE["max1"]:
                        split_max(0)
                    if f["fin"] and t == VE["wo"]:
                        dve.wait_ge(wo_done, count(o + 1))
                        dve.wait_ge(biased, 1)
                        xa = x_all[:, ds(o * KT, KT), :].rearrange("p k d -> p (k d)")
                        nc.vector.tensor_tensor(xa, Mb[1][:, 0:KT * D], xa, op=ALU.add).then_inc(y_done, 1)
                    if f["mx"] and t == RAW_FROM + 15:
                        split_max(1)
                    if f["pre"] and t == VE["cq"]:
                        dve.wait_ge(q_done, count(s + 3))
                        dve.wait_ge(qk_done, count(s + 2))
                        nc.vector.scalar_tensor_tensor(turn1[:, 0, :], Mb[1][:, 0:T], bq_sb[:, 0:1], cos_sb[:, :],
                                                       op0=ALU.add, op1=ALU.mult)
                        nc.vector.scalar_tensor_tensor(turn2[:, 0, :], Mb[1][:, T:2 * T], bqr_sb[:, 0:1], sin_sb[:, :],
                                                       op0=ALU.add, op1=ALU.mult).then_inc(q_rope, 1)
                    if f["pre"] and t == VE["k"]:
                        dve.wait_ge(k_done, count(s + 3))
                        nc.vector.tensor_tensor(turn1[:, 1, :], Mb[1][:, 0:T], cos_sb[:, :], op=ALU.mult)
                        nc.vector.tensor_tensor(turn2[:, 1, :], Mb[1][:, T:2 * T], sin_sb[:, :],
                                                op=ALU.mult).then_inc(k_rope, 1)

                if ffn == "over" and s in FINISHED:
                    tiles = GATHERS[s - 1]
                    dve.wait_ge(gathered[list(GATHERS).index(s - 1)], 16 * (tiles[1] - tiles[0]))
                    dve.wait_ge(y_done, count(s - 1))
                    finish(*FINISHED[s])

            def route():
                seq = [0]

                def then(ins):
                    seq[0] += 1
                    ins.then_inc(rt, 1)
                    dve.wait_ge(rt, seq[0])

                def wide(v):
                    return v[:, :].unsqueeze(2).broadcast_to([P, NT, NE])

                def each(v):
                    return v[:, :].unsqueeze(1).broadcast_to([P, NT, NE])

                dve.wait_ge(w_late, 16 * 24)
                dve.wait_ge(lg_copied, NCH)
                then(nc.vector.tensor_reduce(top[:, :], logits[:, :, :], axis=AX.X, op=ALU.max))
                nc.vector.tensor_tensor(shifted[:, :, :], logits[:, :, :], wide(top), op=ALU.subtract).then_inc(rt_shift, 1)
                then(nc.vector.tensor_tensor(hit[:, :, :], logits[:, :, :], wide(top), op=ALU.is_equal))
                then(nc.vector.tensor_tensor(rank[:, :, :], hit[:, :, :], each(rank_sb), op=ALU.mult))
                then(nc.vector.tensor_reduce(toprank[:, :], rank[:, :, :], axis=AX.X, op=ALU.max))
                then(nc.vector.tensor_tensor(mask[:, :, :], rank[:, :, :], wide(toprank), op=ALU.is_equal))
                nc.vector.tensor_copy(maskb[:, :, :], mask[:, :, :]).then_inc(mask_done, 1)
                dve.wait_ge(rt_pe, 2)
                then(nc.vector.tensor_copy(pre[0][:, :, :], Xb[1][:, 0:NT * NE].rearrange("p (t e) -> p t e", e=NE)))
                for i in range(5):
                    d = 1 << i
                    nc.vector.tensor_copy(pre[i + 1][:, 0:d, :], pre[i][:, 0:d, :])
                    then(nc.vector.tensor_tensor(pre[i + 1][:, d:NT, :], pre[i][:, d:NT, :], pre[i][:, 0:NT - d, :], op=ALU.add))
                v = Xb[0][:, 0:NT * NE].rearrange("p (t e) -> p t e", e=NE)
                nc.vector.tensor_copy(where[:, 0:1, :], v[:, 0:1, :])
                then(nc.vector.tensor_tensor(where[:, 1:NT, :], v[:, 1:NT, :], pre[5][:, 0:NT - 1, :], op=ALU.add))
                then(nc.vector.tensor_tensor(picked[:, :, :], where[:, :, :], mask[:, :, :], op=ALU.mult))
                then(nc.vector.tensor_reduce(place[:, :], picked[:, :, :], axis=AX.X, op=ALU.add))
                then(nc.vector.tensor_tensor(based[:, :, :], mask[:, :, :], each(base_sb), op=ALU.mult))
                then(nc.vector.tensor_reduce(first[:, :], based[:, :, :], axis=AX.X, op=ALU.add))
                then(nc.vector.tensor_scalar(keep[:, :], place[:, :], float(CAP), None, ALU.is_lt))
                then(nc.vector.tensor_tensor(slot[:, :], first[:, :], place[:, :], op=ALU.add))
                then(nc.vector.tensor_tensor(kept_slot[:, :], slot[:, :], keep[:, :], op=ALU.mult))
                nc.vector.tensor_copy(src_u[:, :], kept_slot[:, :])
                then(nc.vector.tensor_tensor(off[:, :], slot[:, :], spare_sb[:, :], op=ALU.subtract))
                then(nc.vector.tensor_tensor(dest[:, :], off[:, :], keep[:, :], op=ALU.mult))
                then(nc.vector.tensor_tensor(dest2[:, :], dest[:, :], spare_sb[:, :], op=ALU.add))
                nc.vector.tensor_copy(dest_u[:, :], dest2[:, :]).then_inc(routed, 1)
                dve.wait_ge(rt_exp, 1)
                then(nc.vector.tensor_reduce(denom[:, :], expl[:, :, :], axis=AX.X, op=ALU.add))
                then(nc.vector.reciprocal(invden[:, :], denom[:, :]))
                then(nc.vector.tensor_tensor(gate[:, :], invden[:, :], keep[:, :], op=ALU.mult))

            def finish(first, last):
                with dve.Fori(first, last) as b:
                    for k in range(KT):
                        t = b * KT + k
                        xa = x_all[:, ds(t, 1), :].rearrange("p a n -> p (a n)")
                        last_one = nc.vector.scalar_tensor_tensor(xa, ffn_all[:, ds(t, 1), :].rearrange("p a n -> p (a n)"),
                                                                  gate[:, ds(t, 1)], xa, op0=ALU.mult, op1=ALU.add)
                    last_one.then_inc(res_done, 1)

            def normalised(c):
                normalise(c, 0)
                normalise(c + 1, 1)
                keep_normalised(c, 0)
                keep_normalised(c + 1, 1)

            normalised(0)
            normalised(2)
            step(-2, 0, None, -1)
            logits_out(0, 0)
            logits_out(1, 1)
            normalised(4)
            step(-1, 1, None, -1)
            logits_out(2, 0)
            logits_out(3, 1)
            normalised(6)
            for c in range(4, NCH):
                logits_out(c, c % 2)
            route()
            run_steps(dve, step)
            dve.wait_ge(gathered[-1], 16 * KT * (B - BATCHES_LAST))
            dve.wait_ge(y_done, B)
            finish(BATCHES_LAST, B)

        @block.tensor
        def _(pe):
            pe.wait_ge(w_early, 32)

            def turn_tokens(c, i):
                pe.wait_ge(xn_done, count(c + 1))
                pe.wait_ge(xT_evac, count(c - 1))
                for k in range(CK):
                    last = nc.tensor.transpose(Sb[i][:, k * P:(k + 1) * P], xn_ring[:, i, k, :], id_sb[:, :])
                last.then_inc(xT_done, 1)

            def router(c, i):
                pe.wait_ge(xT_evac, count(c + 1))
                pe.wait_ge(lg_copied, count(c - 1))
                for k in range(CK):
                    last = nc.tensor.matmul(Xb[i][:, k * NE:(k + 1) * NE], xnT_ring[:, i, k * P:(k + 1) * P], wg_sb[:, :],
                                            start=True, stop=True)
                last.then_inc(lg_done, 1)

            def step(s, par, ffn, u):
                f = has(s)
                other = 1 - par
                p, a, o = s + 2, s - 1, s - 2

                experts_now = count(s - FFN_AFTER + 1, NCH) if ffn == "on" else NCH if ffn == "over" else 0

                def pv(b, slot, g):
                    heads = HEADS[4 * g:4 * g + 4]
                    half, e = g // 2, g % 2
                    done = [i for i in range(NH) if i < 4 * g + 4]
                    pe.wait_ge(exp_done, count(b * NH + len(done)))
                    pe.wait_ge(mul_pool, count(pool_mults(b, len(done))))
                    pe.wait_ge(mul_dve, count(b * len(DVE_HEADS) + sum(i in DVE_HEADS for i in done)))
                    if e == 0:
                        pe.wait_ge(o_evac, count(2 * b + half))
                    for k in range(KT):
                        for j, h in enumerate(heads):
                            last = nc.tensor.matmul(PVb[32 * j:32 * j + 32, half * T:(half + 1) * T],
                                                    Va[slot][:, k, 32 * h:32 * h + 32],
                                                    probs[:, h, k * T:(k + 1) * T],
                                                    start=(e == 0 and k == 0), stop=(e == 1 and k == KT - 1))
                    last.then_inc(pv_done, 1)

                for t in range(SLOTS):
                    if f["attn"]:
                        for n in [n for n in range(NH) if SCORES[n] == t]:
                            e, g = n // GROUP, HEADS[n] % GROUP
                            if n % 8 == 0:
                                pe.wait_ge(mrow_in[n // 8], count(16 * (a + 1)))
                            pe.wait_ge(exp_done, count(16 * a + n - 1))
                            if n in log_heads(a):
                                for i in range(3):
                                    nc.tensor.matmul(Sb[n % 2][:, :], idb_sb[:, :], logd_sb[:, i * KT * T:(i + 1) * KT * T],
                                                     start=(i == 0), stop=False)
                            for k in range(KT):
                                last = nc.tensor.matmul(Sb[n % 2][:, k * T:(k + 1) * T],
                                                        Ks[other][e][:, g, k * P:(k + 1) * P], Qs[other][e][:, g, :],
                                                        start=n not in log_heads(a), stop=n not in log_heads(a) or k == KT - 1)
                            last.then_inc(s_done, 1)
                    if f["mx"] and RAW_FROM <= t < RAW_FROM + 16:
                        i = t - RAW_FROM
                        half, g, q = i // 8, i % 8 // 2 * 2, i % 2
                        if i == 0 and ffn is None:
                            pe.wait_ge(routed, 1)
                        if i % 8 == 0:
                            pe.wait_ge(stack_in[par][half], count(96 * (u + 1)))
                        pe.wait_ge(reduced, count(16 * s + i - 1))
                        for j in range(2):
                            last = nc.tensor.matmul(Xb[i % 2][:, j * T:(j + 1) * T], Qs[par][half][0:MROW, g + j, q * P:(q + 1) * P],
                                                    Ks[par][half][0:MROW, g + j, :], start=True, stop=True)
                        last.then_inc(raw_done, 1)
                    if f["attn"] and t == PE["max2"]:
                        pe.wait_ge(mt_evac, count(2 * s - 1, 2 * B))
                        pe.wait_ge(maxlo, count(2 * s))
                        for k in range(KT):
                            last = nc.tensor.transpose(Mb[2][0:16, k * P // 2:(k + 1) * P // 2].bitcast(bf16),
                                                       maxparts[:, k, 1, :], idb_sb[:, :])
                        last.then_inc(mt_done, 1)
                    if ffn == "on" and t == PE["ex_in"]:
                        pe.wait_ge(k_rope, count(s + 2, B))
                        pe.wait_ge(ex_in, count(16 * (s - FFN_AFTER + 1)))
                        for k in range(CK):
                            last = nc.tensor.transpose(Mb[1][:, k * P:(k + 1) * P], exin[:, k, :], id_sb[:, :])
                        last.then_inc(ft_done, 1)
                    if f["fin"] and t == PE["pv2"]:
                        pv(o, par, 3)
                    if f["fin"] and t == PE["o_turn"]:
                        pe.wait_ge(mt_evac, count(2 * s, 2 * B))
                        pe.wait_ge(o_evac, count(2 * o + 2))
                        for q in range(KT):
                            for half in range(2):
                                at = (2 * q + half) * P
                                last = nc.tensor.transpose(Mb[2][:, at:at + P], Oacc[:, half, q * P:(q + 1) * P], id_sb[:, :])
                        last.then_inc(otr_done, 1)
                    if f["mx"] and t == PE["mem"]:
                        pe.wait_ge(c_evac, count(s + 2, B))
                        pe.wait_ge(v_evac, count(s, B))
                        pe.wait_ge(mk_done, count(s + 1))
                        for k in range(KT):
                            nc.tensor.matmul(Mb[0][:, k * NH:(k + 1) * NH], qk[par][:, 0, k * P:(k + 1) * P], mk[par][:, :],
                                             start=True, stop=True)
                        pe.wait_ge(cmean_done, count(s + 1))
                        nc.tensor.matmul(Mb[0][:, P:2 * P], cmean[par][:, :], wv_sb[:, :], start=True,
                                         stop=True).then_inc(mem_done, 1)
                    if f["fin"] and t == PE["o_back"]:
                        pe.wait_ge(o_ready, count(o + 1))
                        for k in range(KT):
                            last = nc.tensor.transpose(Mb[2][:, k * P:(k + 1) * P],
                                                       Oq[:, k * NH:(k + 1) * NH, :].rearrange("p h d -> p (h d)"), id_sb[:, :])
                        last.then_inc(o2t_done, 1)
                    if ffn == "on" and t == PE["ex_out"]:
                        pe.wait_ge(memo_done, count(s + 1, B))
                        pe.wait_ge(ft_evac, s - FFN_AFTER + 1)
                        for k in range(CK):
                            last = nc.tensor.matmul(Mb[0][:, k * D:(k + 1) * D], exT[:, k * P:(k + 1) * P],
                                                    wet_sb[:, ds((s - FFN_AFTER) * D, D)], start=True, stop=True)
                        last.then_inc(fo_done, 1)
                    if f["mx"] and t == PE["values"]:
                        pe.wait_ge(memo_done, count(s + 1, B))
                        pe.wait_ge(exout_done, experts_now)
                        pe.wait_ge(c_evac, count(s + 1))
                        for k in range(KT):
                            last = nc.tensor.matmul(Mb[0][:, k * P:(k + 1) * P], cT[par][:, k * P:(k + 1) * P], wv_sb[:, :],
                                                    start=True, stop=True)
                        last.then_inc(v_done, 1)
                    if f["fin"] and t == PE["wo"]:
                        pe.wait_ge(k_rope, count(s + 2, B))
                        pe.wait_ge(ft_evac, experts_now)
                        pe.wait_ge(o2t_evac, count(o + 1))
                        for k in range(KT):
                            last = nc.tensor.matmul(Mb[1][:, k * D:(k + 1) * D], OT[:, k * P:(k + 1) * P], wo_sb[:, :],
                                                    start=True, stop=True)
                        last.then_inc(wo_done, 1)
                    if f["mx"] and t == PE["max1"]:
                        pe.wait_ge(mt_evac, count(2 * s, 2 * B))
                        pe.wait_ge(o2t_evac, count(s - 1, B))
                        pe.wait_ge(maxlo, count(2 * s + 1))
                        for k in range(KT):
                            last = nc.tensor.transpose(Mb[2][0:16, k * P // 2:(k + 1) * P // 2].bitcast(bf16),
                                                       maxparts[:, k, 0, :], idb_sb[:, :])
                        last.then_inc(mt_done, 1)
                    if f["pre"] and t == PE["cq"]:
                        xb = xnT[:, ds(p * T, T)]
                        pe.wait_ge(v_evac, count(s + 1, B))
                        pe.wait_ge(c_evac, count(s + 2, B))
                        nc.tensor.matmul(Mb[0][0:LAT, 0:T], wd_sb[:, :], xb, start=True, stop=True).then_inc(c_done, 1)
                        pe.wait_ge(k_rope, count(s + 2, B))
                        pe.wait_ge(y_done, count(s - 1, B))
                        nc.tensor.matmul(Mb[1][:, 0:T], wq_sb[:, :], xb, start=True, stop=True)
                        nc.tensor.matmul(Mb[1][:, T:2 * T], wqr_sb[:, :], xb, start=True, stop=True).then_inc(q_done, 1)
                    if f["pre"] and t == PE["k"]:
                        pe.wait_ge(q_rope, count(s + 3, B))
                        pe.wait_ge(c_evac, count(s + 3))
                        nc.tensor.matmul(Mb[1][:, 0:T], wk_sb[:, :], cT[par][:, :], start=True, stop=True)
                        nc.tensor.matmul(Mb[1][:, T:2 * T], wkr_sb[:, :], cT[par][:, :], start=True,
                                         stop=True).then_inc(k_done, 1)
                    if f["attn"] and t in PV_SLOT:
                        pv(a, other, PV_SLOT.index(t))

            def count_tokens():
                pe.wait_ge(mask_done, 1)
                pe.wait_ge(lg_copied, NCH)
                mb = maskb[:, :, :].rearrange("p t e -> p (t e)")
                nc.tensor.matmul(Xb[0][:, 0:NT * NE], before_sb[:, :], mb, start=True, stop=True).then_inc(rt_pe, 1)
                nc.tensor.matmul(Xb[1][:, 0:NT * NE], onesb_sb[:, :], mb, start=True, stop=True).then_inc(rt_pe, 1)

            turn_tokens(0, 0)
            turn_tokens(1, 1)
            pe.wait_ge(w_late, 16 * 24)
            pe.wait_ge(init_dve, 1)
            pe.wait_ge(xT_evac, 1)
            step(-2, 0, None, -1)
            router(0, 0)
            turn_tokens(2, 0)
            router(1, 1)
            turn_tokens(3, 1)
            step(-1, 1, None, -1)
            with pe.Fori(4, NCH - 1, 2) as c:
                router(c - 2, 0)
                turn_tokens(c, 0)
                router(c - 1, 1)
                turn_tokens(c + 1, 1)
            router(NCH - 2, 0)
            router(NCH - 1, 1)
            pe.wait_ge(init_pool, 2)
            pe.wait_ge(one_rows_in, 64)
            count_tokens()
            pe.wait_ge(xT_evac, NCH)
            run_steps(pe, step)


ROWS = np.arange(P).reshape(2, GROUP, HD).transpose(0, 2, 1).reshape(-1)


def _tables():
    bf = np.dtype("bfloat16")
    f = np.float32
    inv = (f(1.0) / np.power(f(10000.0), np.arange(0, HD, 2, dtype=f) / f(HD))).astype(f)
    freq = np.outer(np.arange(T, dtype=f), inv).astype(f)
    cos, sin = np.cos(freq).astype(f).T, np.sin(freq).astype(f).T
    rope_cos = np.tile(np.concatenate([cos, cos]), (NH, 1))[ROWS]
    rope_sin = np.tile(np.concatenate([-sin, sin]), (NH, 1))[ROWS]
    i = np.arange(T, dtype=np.float64)
    d = i[None, :] - i[:, None]
    dec = np.exp(-0.1 * np.log(np.abs(d) + 1.0)) * (np.exp(-np.maximum(d, 0.0) * 0.01) + 1e-9)
    rest, log_decay = (np.log(dec) / SCALE).reshape(KT, P, T).transpose(1, 0, 2).reshape(P, KT * T), []
    for _ in range(3):
        log_decay.append(rest.astype(bf))
        rest = rest - log_decay[-1].astype(np.float64)
    decay = dec.reshape(KT, P, T).transpose(1, 0, 2).reshape(P, KT * T)
    ident = np.eye(P)
    before = np.triu(np.ones((P, P)), 1)
    head_mean = np.repeat(np.eye(NH), HD, axis=0)[ROWS] / T
    one_rows = np.ones((2, GROUP * T))
    rank = np.tile(np.arange(NE, 0, -1.0), (P, 1))
    base = np.tile(np.arange(NE) * float(CAP), (P, 1))
    spare = NTOK + np.arange(NTOK, dtype=f).reshape(NT, P).T
    c = np.ascontiguousarray
    return [c(rope_cos, f), c(rope_sin, f), c(decay, f), np.concatenate(log_decay, 1), c(ident, f), c(ident).astype(bf), before.astype(bf),
            np.ones((P, P)).astype(bf), c(head_mean, f), one_rows.astype(bf),
            c(rank, f), c(base, f), c(spare, f)]


def kernel(**inputs):
    import concourse.bacc as _bacc
    from concourse import mybir as _mybir
    from concourse.bass_utils import run_bass_kernel_spmd as _run

    a = {k.replace("L0_", ""): np.asarray(v) for k, v in inputs.items()}
    swap = (np.arange(NH * HD).reshape(NH, 2, HD // 2)[:, ::-1]).reshape(-1)[ROWS]
    up = np.concatenate([a["attn_Wkv_up"], a["attn_bkv_up"][None, :]])
    up = up.reshape(LAT + 1, NH, 2, HD)
    wk, wv = up[:, :, 0].reshape(LAT + 1, P), up[:, :, 1].reshape(LAT + 1, P)
    wet = a["ffn_W"].transpose(2, 0, 1).reshape(D, NE * D)
    arrs = [a["attn_x"], a["attn_Wq"][:, ROWS], a["attn_Wq"][:, swap], a["attn_bq"][ROWS][:, None], a["attn_bq"][swap][:, None],
            a["attn_Wkv_down"], a["attn_bkv_down"][:, None], wk[:, ROWS], wk[:, swap], wv, a["attn_Wo"], a["attn_bo"][None, :],
            a["ffn_wg"], wet, a["ffn_b"].reshape(1, NE * D)] + _tables()
    names = ["x", "wq", "wqr", "bq", "bqr", "wd", "bd", "wk", "wkr", "wv", "wo", "bo", "wg", "wet", "be",
             "rope_cos", "rope_sin", "decay", "log_decay", "ident", "identb", "before", "onesb", "head_mean", "one_rows",
             "expert_rank", "expert_base", "spare_slot"]
    nc = _bacc.Bacc("TRN2", target_bir_lowering=False, num_devices=1)
    arrays, args = {}, []
    for name, v in zip(names, arrs):
        v = np.ascontiguousarray(v)
        arrays[f"in_{name}_dram"] = v
        args.append(nc.dram_tensor(f"in_{name}_dram", v.shape, _mybir.dt.from_np(v.dtype), kind="ExternalInput").ap())
    args.append(nc.dram_tensor("out_0_dram", (B, T, D), _mybir.dt.float32, kind="ExternalOutput").ap())
    mixed_block_kernel(nc, *args)
    r = _run(nc, [arrays], core_ids=[0])
    return r.results[0]["out_0_dram"]
```

```python
import numpy as np
import concourse.bass as bass
from concourse import mybir
from contextlib import ExitStack

B, T, D = 16, 256, 128
NH, HD = 16, 8
LAT = 32
NE = 8
P = 128
KT = T // P
NT = B * KT
NTOK = B * T
CAP = NTOK // NE
CK = 4
NCH = NT // CK
GROUP = NH // 2
Q_STACK = ((0, 3), (1, 2), (2, 1))
K_STACK = 3, 2, 1
MROW = 96
HEADS = [0, 2, 4, 6, 1, 3, 5, 7, 8, 10, 12, 14, 9, 11, 13, 15]
DVE_HEADS = (2, 6, 9, 11)
PE_HEADS = (4,)
X_LOADS = 0, CK, 2 * CK, 5 * CK, NT
STAT_PARTS = (0, 2 * CK), (2 * CK, NT)
FFN_AFTER = 3
SCATTERS = {0: (0, 18), 1: (18, 25), 2: (25, NT)}
GATHERS = {12: (0, 6), 13: (6, 12), 14: (12, 18), 15: (18, 24), 16: (24, NT)}
MORE_PE_HEADS = (1, 5, 8, 12, 13)
SLOTS = 18
SCORES = (0, 1, 1, 2, 3, 4, 5, 6, 7, 8, 9, 10, 11, 12, 13, 14)
RAW_FROM = 1
DVE_SLOT = (4, 8, 10, 13)
PV_SLOT = (7, 11, 15)
PE = dict(max2=2, ex_in=6, pv2=4, o_turn=5, mem=6, o_back=8, ex_out=9, values=12, wo=11, max1=12, cq=14, k=16)
EV = dict(max2=2, part1=1, part2=5, ex_in=7, pv2=4, mem=6, o_back=9, values=12, max1=12, pv1=13, cq=14)
VE = dict(means=4, o_turn=6, mem=7, ex_out=10, max1=10, wo=12, cq=14, k=17, finish=16)
POOL_QK, POOL_REST, POOL_PART3 = 0, 1, 4
SCALE = float(1.0 / np.sqrt(np.float32(HD)))
LN_EPS = 1e-5


def mixed_block_kernel(nc, x, wq, wqr, bq, bqr, wd, bd, wk, wkr, wv, wo, bo, wg, wet, be,
                       rope_cos, rope_sin, decay, log_decay, ident, identb, before, onesb, head_mean, one_rows,
                       expert_rank, expert_base, spare_slot, out):
    f32, bf16, u32 = mybir.dt.float32, mybir.dt.bfloat16, mybir.dt.uint32
    ALU, ACT, AX = mybir.AluOpType, mybir.ActivationFunctionType, mybir.AxisListType
    ds = bass.ds

    ctx = ExitStack()
    with ctx:
        def sb(name, shape, dt=f32):
            return ctx.enter_context(nc.sbuf_tensor(name, shape, dt))

        def sem(name):
            return ctx.enter_context(nc.semaphore(name))

        parts_dram = nc.dram_tensor("parts_dram", (2, 3, 2, P, T), bf16, kind="Internal").ap()
        slots_in = nc.dram_tensor("slots_in", (2 * NTOK, D), f32, kind="Internal").ap()
        max_dram = [nc.dram_tensor(f"max_dram{i}", (2, GROUP, T), bf16, kind="Internal").ap() for i in range(2)]
        slots_out = nc.dram_tensor("slots_out", (NTOK, D), f32, kind="Internal").ap()

        wq_sb, wqr_sb = sb("wq_sb", [D, P]), sb("wqr_sb", [D, P])
        bq_sb, bqr_sb, bd_sb = sb("bq_sb", [P, 1]), sb("bqr_sb", [P, 1]), sb("bd_sb", [LAT, 1])
        wd_sb = sb("wd_sb", [D, LAT])
        wk_sb, wkr_sb, wv_sb = sb("wk_sb", [LAT + 1, P]), sb("wkr_sb", [LAT + 1, P]), sb("wv_sb", [LAT + 1, P])
        wo_sb, bo_sb = sb("wo_sb", [P, D]), sb("bo_sb", [P, D])
        wg_sb, wet_sb, be_sb = sb("wg_sb", [D, NE]), sb("wet_sb", [D, NE * D]), sb("be_sb", [P, NE * D])
        cos_sb, sin_sb = sb("cos_sb", [P, T]), sb("sin_sb", [P, T])
        decay_sb, logd_sb = sb("decay_sb", [P, KT * T]), sb("logd_sb", [P, 3 * KT * T], bf16)
        id_sb, idb_sb = sb("id_sb", [P, P]), sb("idb_sb", [P, P], bf16)
        before_sb, onesb_sb = sb("before_sb", [P, P], bf16), sb("onesb_sb", [P, P], bf16)
        hmean_sb = sb("hmean_sb", [P, NH])
        rank_sb, base_sb, spare_sb = sb("rank_sb", [P, NE]), sb("base_sb", [P, NE]), sb("spare_sb", [P, NT])

        x_all = sb("x_all", [P, NT, D])
        xn_all = sb("xn_all", [P, NT, D])
        xnT = sb("xnT", [D, NTOK])
        ffn_all = sb("ffn_all", [P, NT, D])
        stats = sb("stats", [P, NT, 6])
        mean2, mgap, mgap2, msq, ssq, mean, var = (sb(n, [P, NT]) for n in ("mean2", "mgap", "mgap2", "msq", "ssq", "mean", "var"))
        std, rstd, eps_sb = sb("std", [P, NT]), sb("rstd", [P, NT]), sb("eps_sb", [P, 1])
        logits, hit, rank, mask = (sb(n, [P, NT, NE]) for n in ("logits", "hit", "rank", "mask"))
        maskb = sb("maskb", [P, NT, NE], bf16)
        shifted, expl = sb("shifted", [P, NT, NE]), sb("expl", [P, NT, NE])
        pre = [sb(f"pre{i}", [P, NT, NE]) for i in range(6)]
        where, picked, based = sb("where", [P, NT, NE]), sb("picked", [P, NT, NE]), sb("based", [P, NT, NE])
        top, toprank, denom, invden, gate = (sb(n, [P, NT]) for n in ("top", "toprank", "denom", "invden", "gate"))
        place, first, keep, slot, off, dest = (sb(n, [P, NT]) for n in ("place", "first", "keep", "slot", "off", "dest"))
        kept_slot, dest2 = sb("kept_slot", [P, NT]), sb("dest2", [P, NT])
        dest_u, src_u = sb("dest_u", [P, NT], u32), sb("src_u", [P, NT], u32)
        cT = [sb(f"cT{i}", [LAT + 1, T]) for i in range(2)]
        turn1, turn2 = sb("turn1", [P, 2, T]), sb("turn2", [P, 2, T])
        qk = [sb(f"qk{i}", [P, 2, T]) for i in range(2)]
        part = [sb(f"part{i}", [P, 2, T], bf16) for i in range(3)]
        rest = sb("rest", [P, 2, T])
        ksum = [sb(f"ksum{i}", [P, 1]) for i in range(2)]
        mk = [sb(f"mk{i}", [P, NH]) for i in range(2)]
        csum = [sb(f"csum{i}", [LAT, 1]) for i in range(2)]
        cmean = [sb(f"cmean{i}", [LAT + 1, P]) for i in range(2)]
        ones_lat = sb("ones_lat", [LAT, P])
        Qs = [[sb(f"Qs{i}_{e}", [P, GROUP, T], bf16) for e in range(2)] for i in range(2)]
        Ks = [[sb(f"Ks{i}_{e}", [P, GROUP, T], bf16) for e in range(2)] for i in range(2)]
        Va = [sb(f"Va{i}", [P, KT, NH * 32]) for i in range(2)]
        negmax = [sb(f"negmax{i}", [P, KT, NH]) for i in range(2)]
        maxparts = sb("maxparts", [P, KT, 2, 16], bf16)
        maxT = [sb(f"maxT{i}", [16, T], bf16) for i in range(2)]
        probs = sb("probs", [P, NH, KT * T])
        Oacc = sb("Oacc", [P, 2, T])
        rden, Oq, OT = sb("rden", [P, 2 * NH]), sb("Oq", [P, 2 * NH, HD]), sb("OT", [P, T])
        Oraw = sb("Oraw", [P, 2 * NH, HD])
        th, gth = sb("th", [P, 2 * NH]), sb("gth", [P, 2 * NH])
        memo = [sb(f"memo{i}", [P, 2 * NH, HD]) for i in range(2)]
        exin, exT, exout = sb("exin", [P, CK, D]), sb("exT", [D, CK * P]), sb("exout", [P, CK, D])

        def bank(name):
            return ctx.enter_context(nc.psum_tensor(name, [P, 512], f32))

        Sb = [bank(f"scores{i}") for i in range(2)]
        Xb = [bank(f"raw{i}") for i in range(2)]
        PVb = bank("pv")
        Mb = [bank(f"misc{i}") for i in range(3)]

        w_early = sem("w_early")
        w_proj = sem("w_proj")
        w_late = sem("w_late")
        biased = sem("biased")
        zeroed = sem("zeroed")
        one_rows_in = sem("one_rows_in")
        init_dve = sem("init_dve")
        init_pool = sem("init_pool")
        init_ffn = sem("init_ffn")
        stat = sem("stat")
        joined = sem("joined")
        var_done = sem("var_done")
        std_done = sem("std_done")
        rstd_done = sem("rstd_done")
        xn_done = sem("xn_done")
        xT_done = sem("xT_done")
        xT_evac = sem("xT_evac")
        lg_done = sem("lg_done")
        lg_copied = sem("lg_copied")
        rt = sem("rt")
        rt_pe = sem("rt_pe")
        rt_exp = sem("rt_exp")
        rt_shift = sem("rt_shift")
        mask_done = sem("mask_done")
        routed = sem("routed")
        scattered = sem("scattered")
        c_done = sem("c_done")
        q_done = sem("q_done")
        mt_done = sem("mt_done")
        v_done = sem("v_done")
        k_done = sem("k_done")
        otr_done = sem("otr_done")
        mem_done = sem("mem_done")
        ft_done = sem("ft_done")
        o2t_done = sem("o2t_done")
        fo_done = sem("fo_done")
        wo_done = sem("wo_done")
        c_evac = sem("c_evac")
        q_rope = sem("q_rope")
        mt_evac = sem("mt_evac")
        v_evac = sem("v_evac")
        k_rope = sem("k_rope")
        o_raw = sem("o_raw")
        rden_done = sem("rden_done")
        th_done = sem("th_done")
        gth_done = sem("gth_done")
        memo_done = sem("memo_done")
        mk_done = sem("mk_done")
        cmean_done = sem("cmean_done")
        o_ready = sem("o_ready")
        ft_evac = sem("ft_evac")
        o2t_evac = sem("o2t_evac")
        exout_done = sem("exout_done")
        y_done = sem("y_done")
        qk_done = sem("qk_done")
        rest_done = sem("rest_done")
        parts_out = sem("parts_out")
        raw_done = sem("raw_done")
        reduced = sem("reduced")
        maxhi = sem("maxhi")
        maxlo = sem("maxlo")
        s_done = sem("s_done")
        exp_done = sem("exp_done")
        mul_dve = sem("mul_dve")
        mul_pool = sem("mul_pool")
        pv_done = sem("pv_done")
        o_evac = sem("o_evac")
        ex_in = sem("ex_in")
        ex_stored = sem("ex_stored")
        gathered = [sem(f"gathered{i}") for i in range(len(GATHERS))]
        res_done = sem("res_done")
        out_done = sem("out_done")
        x_in = [sem(f"x_in{i}") for i in range(len(X_LOADS) - 1)]
        mrow_in = [sem(f"mrow_in{i}") for i in range(2)]
        max_out = [sem(f"max_out{i}") for i in range(2)]
        stack_in = [[sem(f"stack_in{i}_{e}") for e in range(2)] for i in range(2)]
        part_done = [sem(f"part_done{i}") for i in range(3)]
        block = ctx.enter_context(nc.Block())

        FINISHED = {s + 1: (first // KT, min(last // KT, B - 1)) for s, (first, last) in GATHERS.items()}
        def log_heads(b):
            return PE_HEADS + (MORE_PE_HEADS if isinstance(b, int) and not 2 <= b < 2 + NCH else ())

        def pool_heads(b):
            return [i for i in range(NH) if i not in DVE_HEADS + log_heads(b)]

        def pool_mults(b, places):
            if isinstance(b, int):
                before = sum(len(pool_heads(j)) for j in range(b))
            else:
                before = (b - 2) * len(pool_heads(b)) + sum(len(pool_heads(j)) for j in range(2))
            return before + sum(i < places for i in pool_heads(b))

        def count(n, most=None):
            if not isinstance(n, int):
                return n
            return max(0, n if most is None else min(n, most))

        def values_of(i, k):
            v = Va[i][:, k, :]
            return bass.AP(v.tensor, v.offset, [v.ap[0], (64, GROUP), (48, 2), (1, HD)])

        def has(s):
            if not isinstance(s, int):
                return dict(pre=True, proj=True, mx=True, attn=True, fin=True)
            return dict(pre=s + 2 < B, proj=-1 <= s < B - 1, mx=0 <= s < B, attn=0 <= s - 1 < B, fin=0 <= s - 2 < B)

        def run_steps(eng, step, from_step=0):
            if from_step == 0:
                step(0, 0, None, 0)
            step(1, 1, None, 0)
            step(2, 0, None, 1)
            step(3, 1, "on", 1)
            with eng.Fori(2, (NCH + FFN_AFTER - 1) // 2) as u:
                step(2 * u, 0, "on", u)
                step(2 * u + 1, 1, "on", u)
            for s in range(NCH + FFN_AFTER - 1, B + 2):
                step(s, s % 2, "on" if s < NCH + FFN_AFTER else "over", s // 2)

        @block.sync
        def _(sp):
            xv = x.rearrange("b (k p) d -> p (b k) d", p=P)
            for i, (first, last) in enumerate(zip(X_LOADS, X_LOADS[1:])):
                sp.dma_start(x_all[:, first:last, :], xv[:, first:last, :]).then_inc(x_in[i], 16)
            proj = [(wq_sb, wq), (wqr_sb, wqr), (bq_sb, bq), (bqr_sb, bqr), (wd_sb, wd), (bd_sb, bd), (wk_sb, wk),
                    (wkr_sb, wkr), (wv_sb, wv), (cos_sb, rope_cos), (sin_sb, rope_sin)]
            for to, src in proj:
                sp.dma_start(to[:, :], src).then_inc(w_proj, 16)
            late = [(idb_sb, identb),
                    (before_sb, before), (onesb_sb, onesb), (hmean_sb, head_mean),
                    (rank_sb, expert_rank), (base_sb, expert_base), (spare_sb, spare_slot), (decay_sb, decay), (logd_sb, log_decay),
                    (wo_sb, wo), (bo_sb, bo.broadcast_to([P, D])), (wet_sb, wet), (be_sb, be.broadcast_to([P, NE * D]))]
            for to, src in late:
                sp.dma_start(to[:, :], src).then_inc(w_late, 16)
            sp.wait_ge(init_pool, 1)
            for i in range(2):
                for e in range(2):
                    sp.dma_start(Ks[i][e][MROW:MROW + 2, :, :].rearrange("p g t -> p (g t)"), one_rows).then_inc(one_rows_in, 16)
            sp.wait_ge(init_ffn, 1)
            sp.dma_start(slots_in[0:NTOK, :].rearrange("(a p) d -> p a d", p=P), ffn_all[:, :, :]).then_inc(zeroed, 16)

            def held(n):
                return n if isinstance(n, int) else sp.snap(sp.to_reg(n), min_val=1)

            def stack(par, e, j):
                row = GROUP * T
                one_part = 2 * P * T
                times, nk = Q_STACK[j][1], K_STACK[j]
                at = HD * sum(t for _, t in Q_STACK[:j])
                rows = times * HD
                src = parts_dram[par, j, 0, e * P // 2:(e + 1) * P // 2, :]
                q_src = bass.AP(src.tensor, src.offset, [(0, times), (row, HD), (1, row)])
                sp.dma_start(Qs[par][e][at:at + rows, :, :].rearrange("p g t -> p (g t)"),
                             q_src).then_inc(stack_in[par][e], 16)
                src = parts_dram[par, 0, 1, e * P // 2:(e + 1) * P // 2, :]
                k_src = bass.AP(src.tensor, src.offset, [(one_part, nk), (row, HD), (1, row)])
                sp.dma_start(Ks[par][e][at:at + rows, :, :].rearrange("p g t -> p (g t)"),
                             k_src).then_inc(stack_in[par][e], 16)

            def max_rows_out(half):
                sp.dma_start(max_dram[half].rearrange("r g t -> (r g) t"), maxT[half][:, :]).then_inc(max_out[half], 16)

            def max_rows_in(half, par):
                sp.dma_start(Qs[par][half][MROW:MROW + 2, :, :], max_dram[half]).then_inc(mrow_in[half], 16)

            ov = out.rearrange("b (k p) d -> p (b k) d", p=P)

            def outputs(first, last):
                with sp.Fori(first, last) as b:
                    sp.wait_ge(res_done, count(b + 1))
                    sp.dma_start(ov[:, ds(b * KT, KT), :], x_all[:, ds(b * KT, KT), :]).then_inc(out_done, 16)

            def step(s, par, ffn, u):
                f = has(s)
                other = 1 - par
                c = s - FFN_AFTER
                at = {k: held(v) for k, v in (
                    ("c", c), ("c+1", c + 1), ("s+2", s + 2), ("2s", 2 * s), ("2s+1", 2 * s + 1), ("48s+96", 48 * s + 96), ("16s", 16 * s), ("16s-8", 16 * s - 8), ("16s+16", 16 * s + 16))}
                if ffn == "on":
                    first = held(c * (CK * P))
                    sp.wait_ge(scattered, 16 * NT)
                    sp.wait_ge(ft_done, count(at["c"]))
                    sp.dma_start(exin[:, :, :], slots_in[ds(first, CK * P), :].rearrange("(k p) d -> p k d", p=P)
                                 ).then_inc(ex_in, 16)
                if f["attn"]:
                    sp.wait_ge(mt_evac, count(at["2s"]))
                    max_rows_out(1)
                if f["proj"]:
                    sp.wait_ge(part_done[0], count(at["s+2"]))
                    sp.dma_start(parts_dram[other, 0].rearrange("t p n -> p t n"), part[0][:, :, :]).then_inc(parts_out, 16)
                if f["attn"]:
                    sp.wait_ge(max_out[1], count(at["16s"]))
                    max_rows_in(1, other)
                if f["proj"]:
                    for i in (1, 2):
                        sp.wait_ge(part_done[i], count(at["s+2"]))
                        sp.dma_start(parts_dram[other, i].rearrange("t p n -> p t n"), part[i][:, :, :]).then_inc(parts_out, 16)
                    sp.wait_ge(parts_out, count(at["48s+96"]))
                    if f["attn"]:
                        sp.wait_ge(s_done, count(at["16s-8"]))
                    else:
                        sp.wait_ge(init_pool, 1)
                    stack(other, 0, 0)
                    stack(other, 0, 1)
                    stack(other, 0, 2)
                if f["mx"]:
                    sp.wait_ge(mt_evac, count(at["2s+1"]))
                    max_rows_out(0)
                    sp.wait_ge(max_out[0], count(at["16s+16"]))
                    max_rows_in(0, par)
                if f["proj"]:
                    if f["attn"]:
                        sp.wait_ge(s_done, count(at["16s"]))
                    stack(other, 1, 0)
                    stack(other, 1, 1)
                    stack(other, 1, 2)
                if ffn == "on":
                    sp.wait_ge(exout_done, count(at["c+1"]))
                    sp.dma_start(slots_out[ds(first, CK * P), :].rearrange("(k p) d -> p k d", p=P), exout[:, :, :]
                                 ).then_inc(ex_stored, 16)
                if ffn == "over" and s - 1 in FINISHED:
                    outputs(*FINISHED[s - 1])

            step(-2, 0, None, -1)
            step(-1, 1, None, -1)
            run_steps(sp, step)
            outputs(FINISHED[B + 1][0], B)
            sp.wait_ge(out_done, 16 * B)

        @block.gpsimd
        def _(pool):
            for i in range(2):
                nc.gpsimd.memset(Va[i][:, :, :], 0.0)
                for half in range(2):
                    nc.gpsimd.memset(Qs[i][half][:, :, :].rearrange("p g t -> p (g t)").bitcast(u32), 0)
                    last = nc.gpsimd.memset(Ks[i][half][:, :, :].rearrange("p g t -> p (g t)").bitcast(u32), 0)
            last.then_inc(init_pool, 1)
            pool.wait_ge(init_pool, 1)
            nc.gpsimd.memset(ffn_all[:, :, :], 0.0).then_inc(init_ffn, 1)
            for i in range(2):
                v = Va[i][:, :, :].rearrange("p k (g s r) -> p (k g) s r", s=2, r=32)
                nc.gpsimd.memset(v[:, :, 0, 8:9], 1.0)
                last = nc.gpsimd.memset(v[:, :, 1, 24:25], 1.0)
            last.then_inc(init_pool, 1)

            def scatter(t):
                nc.gpsimd.indirect_dma_start(
                    out=slots_in[:, :], out_offset=bass.IndirectOffsetOnAxis(ap=dest_u[:, t:t + 1], axis=0),
                    in_=xn_all[:, t, :], in_offset=None).then_inc(scattered, 16)

            def gather(t, done):
                nc.gpsimd.indirect_dma_start(
                    out=ffn_all[:, t, :], out_offset=None, in_=slots_out[:, :],
                    in_offset=bass.IndirectOffsetOnAxis(ap=src_u[:, t:t + 1], axis=0)).then_inc(done, 16)

            def step(s, par, ffn, u):
                f = has(s)
                other = 1 - par
                first, last = (0, 0) if ffn == "on" or s < 1 else SCATTERS.get(s) or GATHERS.get(s) or (0, 0)
                if ffn == "over" and s in GATHERS:
                    pool.wait_ge(ex_stored, 16 * NCH)
                for i in range(NH):
                    if first + i < last and ffn is None:
                        scatter(first + i)
                    if first + i < last and ffn == "over":
                        gather(first + i, gathered[list(GATHERS).index(s)])
                    if f["proj"] and i == POOL_QK:
                        p = s + 1
                        pool.wait_ge(q_rope, count(p + 1))
                        pool.wait_ge(k_rope, count(p + 1))
                        pool.wait_ge(mem_done, count(p - 1))
                        nc.gpsimd.tensor_tensor(qk[other][:, :, :], turn1[:, :, :], turn2[:, :, :],
                                                op=ALU.add).then_inc(qk_done, 1)
                    if f["attn"] and i in pool_heads(s - 1):
                        a, h = s - 1, HEADS[i]
                        pool.wait_ge(exp_done, count(16 * a + i + 1))
                        nc.gpsimd.tensor_tensor(probs[:, h, :], probs[:, h, :], decay_sb[:, :],
                                                op=ALU.mult).then_inc(mul_pool, 1)
                    if f["proj"] and i == POOL_REST:
                        pool.wait_ge(part_done[0], count(p + 1))
                        pool.wait_ge(qk_done, count(p + 1))
                        nc.gpsimd.tensor_tensor(rest[:, :, :], qk[other][:, :, :], part[0][:, :, :],
                                                op=ALU.subtract).then_inc(rest_done, 1)
                    if f["proj"] and i == POOL_PART3:
                        pool.wait_ge(part_done[1], count(p + 1))
                        pool.wait_ge(rest_done, count(p + 1))
                        pool.wait_ge(parts_out, count(48 * p))
                        nc.gpsimd.tensor_tensor(part[2][:, :, :], rest[:, :, :], part[1][:, :, :],
                                                op=ALU.subtract).then_inc(part_done[2], 1)

            step(-2, 0, None, -1)
            step(-1, 1, None, -1)
            pool.wait_ge(xn_done, NCH)
            pool.wait_ge(w_late, 16 * 13)
            nc.gpsimd.tensor_tensor(x_all[:, :, :], x_all[:, :, :], bo_sb[:, :].unsqueeze(1).broadcast_to([P, NT, D]),
                                    op=ALU.add).then_inc(biased, 1)
            step(0, 0, None, 0)
            pool.wait_ge(routed, 1)
            pool.wait_ge(zeroed, 16)
            for t in range(*SCATTERS[0]):
                scatter(t)
            run_steps(pool, step, from_step=1)
            for i, (first, last) in enumerate(GATHERS.values()):
                pool.wait_ge(gathered[i], 16 * (last - first))

        @block.scalar
        def _(act):
            for to, src in ((id_sb, ident), (wg_sb, wg)):
                act.dma_start(to[:, :], src).then_inc(w_early, 16)
            act.wait_ge(init_dve, 1)

            def deviation(part):
                at = slice(*STAT_PARTS[part])
                act.wait_ge(var_done, part + 1)
                nc.scalar.activation(std[:, at], var[:, at], ACT.Sqrt, bias=eps_sb[:, 0:1]).then_inc(std_done, 1)

            def xT_out(c):
                act.wait_ge(xT_done, c + 1)
                nc.scalar.activation(xnT[:, c * CK * P:(c + 1) * CK * P], Sb[c % 2][:, :], ACT.Identity).then_inc(xT_evac, 1)

            def step(s, par, ffn, u):
                f = has(s)
                other = 1 - par
                p, a, o = s + 1, s - 1, s - 2
                for t in range(SLOTS):
                    if f["attn"]:
                        for i in [i for i in range(NH) if SCORES[i] == t]:
                            h = HEADS[i]
                            act.wait_ge(s_done, count(16 * a + i + 1))
                            if i % 4 == 0:
                                act.wait_ge(pv_done, count(4 * (a - 1) + i // 4 + 1))
                            nc.scalar.activation(probs[:, h, :], Sb[i % 2][:, :], ACT.Exp,
                                                 scale=SCALE).then_inc(exp_done, 1)
                    if f["attn"] and t == EV["max2"]:
                        act.wait_ge(mt_done, count(2 * s))
                        act.wait_ge(mrow_in[1], count(16 * a))
                        nc.scalar.activation(maxT[1][:, :], Mb[2][0:16, 0:T // 2].bitcast(bf16),
                                             ACT.Identity).then_inc(mt_evac, 1)
                    if f["proj"] and t == EV["part1"]:
                        act.wait_ge(qk_done, count(p + 1))
                        act.wait_ge(parts_out, count(48 * p))
                        nc.scalar.activation(part[0][:, 0, :], qk[other][:, 0, :], ACT.Identity)
                        act.wait_ge(mk_done, count(p - 1))
                        nc.scalar.activation(part[0][:, 1, :], qk[other][:, 1, :], ACT.Identity,
                                             accum_out=ksum[other][:, 0:1]).then_inc(part_done[0], 1)
                    if ffn == "on" and t == EV["ex_in"]:
                        act.wait_ge(ft_done, s - FFN_AFTER + 1)
                        nc.scalar.activation(exT[:, :], Mb[1][:, :], ACT.Identity).then_inc(ft_evac, 1)
                    if f["fin"] and t == EV["pv2"]:
                        act.wait_ge(pv_done, count(4 * o + 4))
                        nc.scalar.activation(Oacc[:, 1, :], PVb[:, T:2 * T], ACT.Identity).then_inc(o_evac, 1)
                    if f["proj"] and t == EV["part2"]:
                        act.wait_ge(rest_done, count(p + 1))
                        nc.scalar.activation(part[1][:, :, :], rest[:, :, :], ACT.Identity).then_inc(part_done[1], 1)
                    if f["mx"] and t == EV["mem"]:
                        act.wait_ge(mem_done, count(s + 1))
                        act.wait_ge(gth_done, count(s))
                        nc.scalar.activation(th[:, :], Mb[0][:, 0:2 * NH], ACT.Tanh, scale=0.5).then_inc(th_done, 1)
                    if f["fin"] and t == EV["o_back"]:
                        act.wait_ge(o2t_done, count(o + 1))
                        nc.scalar.activation(OT[:, :], Mb[2][:, 0:T], ACT.Identity).then_inc(o2t_evac, 1)
                    if f["mx"] and t == EV["values"]:
                        act.wait_ge(v_done, count(s + 1))
                        act.wait_ge(pv_done, count(4 * (s - 1)))
                        for k in range(KT):
                            last = nc.scalar.activation(values_of(par, k),
                                                        Mb[0][:, k * P:(k + 1) * P].rearrange("p (g e d) -> p g e d", e=2, d=HD),
                                                        ACT.Identity)
                        last.then_inc(v_evac, 1)
                    if f["mx"] and t == EV["max1"]:
                        act.wait_ge(mt_done, count(2 * s + 1))
                        act.wait_ge(mrow_in[0], count(16 * s))
                        nc.scalar.activation(maxT[0][:, :], Mb[2][0:16, 0:T // 2].bitcast(bf16),
                                             ACT.Identity).then_inc(mt_evac, 1)
                    if f["pre"] and t == EV["cq"]:
                        act.wait_ge(c_done, count(s + 3))
                        act.wait_ge(cmean_done, count(s + 1))
                        nc.scalar.activation(cT[par][0:LAT, :], Mb[0][0:LAT, 0:T], ACT.Identity,
                                             bias=bd_sb[:, 0:1], accum_out=csum[par][:, 0:1]).then_inc(c_evac, 1)
                    if f["attn"] and t == EV["pv1"]:
                        act.wait_ge(pv_done, count(4 * a + 2))
                        act.wait_ge(otr_done, count(a))
                        nc.scalar.activation(Oacc[:, 0, :], PVb[:, 0:T], ACT.Identity).then_inc(o_evac, 1)

            def gate_exp():
                act.wait_ge(rt_shift, 1)
                nc.scalar.activation(expl[:, :, :], shifted[:, :, :], ACT.Exp).then_inc(rt_exp, 1)

            deviation(0)
            xT_out(0)
            xT_out(1)
            deviation(1)
            act.wait_ge(w_proj, 16 * 11)
            act.wait_ge(init_pool, 2)
            step(-2, 0, None, -1)
            xT_out(2)
            xT_out(3)
            step(-1, 1, None, -1)
            for c in range(4, NCH):
                xT_out(c)
            gate_exp()
            run_steps(act, step)

        @block.vector
        def _(dve):
            for i in range(2):
                nc.vector.memset(cT[i][LAT:LAT + 1, :], 1.0)
                nc.vector.memset(cmean[i][LAT:LAT + 1, :], 1.0)
            nc.vector.memset(ones_lat[:, :], 1.0)
            nc.vector.memset(eps_sb[:, :], LN_EPS).then_inc(init_dve, 1)

            def tile_stats(t):
                nc.vector.bn_stats(stats[:, ds(t, 1), :].rearrange("p a n -> p (a n)"),
                                   x_all[:, ds(t, 1), :].rearrange("p a n -> p (a n)")).then_inc(stat, 1)

            def stats_of(part):
                first, last = STAT_PARTS[part]
                for i in range(len(x_in)):
                    if first <= X_LOADS[i] < last:
                        dve.wait_ge(x_in[i], 16)
                        with dve.Fori(X_LOADS[i], X_LOADS[i + 1] - CK + 1, CK) as t:
                            for k in range(CK):
                                tile_stats(t + k)
                at = slice(first, last)
                dve.wait_ge(stat, last)
                nc.vector.tensor_tensor(mean2[:, at], stats[:, at, 1], stats[:, at, 4], op=ALU.add)
                nc.vector.tensor_tensor(mgap[:, at], stats[:, at, 1], stats[:, at, 4], op=ALU.subtract)
                nc.vector.tensor_tensor(ssq[:, at], stats[:, at, 2], stats[:, at, 5], op=ALU.add).then_inc(joined, 1)
                dve.wait_ge(joined, 3 * part + 1)
                nc.vector.tensor_scalar(mean[:, at], mean2[:, at], 0.5, None, ALU.mult)
                nc.vector.tensor_scalar(mgap2[:, at], mgap[:, at], 0.5, None, ALU.mult).then_inc(joined, 1)
                dve.wait_ge(joined, 3 * part + 2)
                nc.vector.tensor_tensor(msq[:, at], mgap2[:, at], mgap2[:, at], op=ALU.mult).then_inc(joined, 1)
                dve.wait_ge(joined, 3 * part + 3)
                nc.vector.scalar_tensor_tensor(var[:, at], ssq[:, at], 1.0 / D, msq[:, at], op0=ALU.mult,
                                               op1=ALU.add).then_inc(var_done, 1)
                dve.wait_ge(std_done, part + 1)
                nc.vector.reciprocal(rstd[:, at], std[:, at]).then_inc(rstd_done, 1)
                dve.wait_ge(rstd_done, part + 1)

            def normalise(c):
                for t in range(c * CK, c * CK + CK):
                    last = nc.vector.tensor_scalar(xn_all[:, t, :], x_all[:, t, :], mean[:, t:t + 1], rstd[:, t:t + 1],
                                                   ALU.subtract, ALU.mult)
                last.then_inc(xn_done, 1)

            def logits_out(c):
                dve.wait_ge(lg_done, count(c + 1))
                nc.vector.tensor_copy(logits[:, c * CK:(c + 1) * CK, :].rearrange("p k e -> p (k e)"),
                                      Xb[c % 2][:, 0:CK * NE]).then_inc(lg_copied, 1)

            def step(s, par, ffn, u):
                f = has(s)
                other = 1 - par
                p, a, o = s + 1, s - 1, s - 2

                def split_max(half):
                    n = 8 * half + 8
                    src = negmax[par][:, :, 8 * half:8 * half + 8]
                    to = maxparts[:, :, half, :].rearrange("p k (l g) -> p k l g", l=2)
                    dve.wait_ge(reduced, count(16 * s + n))
                    dve.wait_ge(mt_done, count(2 * s + half - 1))
                    nc.vector.tensor_copy(to[:, :, 0, :], src).then_inc(maxhi, 1)
                    dve.wait_ge(maxhi, count(2 * s + half + 1))
                    nc.vector.tensor_tensor(to[:, :, 1, :], src, to[:, :, 0, :],
                                            op=ALU.subtract).then_inc(maxlo, 1)

                for t in range(SLOTS):
                    i = t - RAW_FROM
                    if f["mx"] and 0 <= i < 16:
                        g, qt = i // 2, i % 2
                        dve.wait_ge(raw_done, count(16 * s + i + 1))
                        nc.vector.tensor_reduce(negmax[par][:, qt, 2 * g:2 * g + 2],
                                                Xb[i % 2][:, :].rearrange("p (h k) -> p h k", h=2),
                                                axis=AX.X, op=ALU.max, negate=True).then_inc(reduced, 1)
                    if f["mx"] and t == VE["means"]:
                        dve.wait_ge(part_done[0], count(s + 1))
                        dve.wait_ge(c_evac, count(s + 1))
                        dve.wait_ge(mem_done, count(s - 1))
                        nc.vector.tensor_scalar(mk[par][:, :], hmean_sb[:, :], ksum[par][:, 0:1], None,
                                                ALU.mult).then_inc(mk_done, 1)
                        nc.vector.tensor_scalar(cmean[par][0:LAT, :], ones_lat[:, :], csum[par][:, 0:1], 1.0 / T,
                                                ALU.mult, ALU.mult).then_inc(cmean_done, 1)
                    if f["fin"] and t == VE["o_turn"]:
                        dve.wait_ge(otr_done, count(o + 1))
                        dve.wait_ge(o_ready, count(o))
                        otr = Mb[2][:, :].rearrange("p (h r) -> p h r", r=2 * HD)
                        nc.vector.reciprocal(rden[:, :], otr[:, :, HD]).then_inc(rden_done, 1)
                        dve.wait_ge(rden_done, count(o + 1))
                        nc.vector.tensor_tensor(Oraw[:, :, :], otr[:, :, 0:HD],
                                                rden[:, :].unsqueeze(2).broadcast_to([P, 2 * NH, HD]),
                                                op=ALU.mult).then_inc(o_raw, 1)
                        dve.wait_ge(o_raw, count(o + 1))
                        dve.wait_ge(memo_done, count(o + 1))
                        dve.wait_ge(o2t_done, count(o))
                        nc.vector.tensor_tensor(Oq[:, :, :], Oraw[:, :, :], memo[par][:, :, :],
                                                op=ALU.add).then_inc(o_ready, 1)
                    if f["mx"] and t == VE["mem"]:
                        dve.wait_ge(th_done, count(s + 1))
                        dve.wait_ge(memo_done, count(s))
                        nc.vector.tensor_scalar(gth[:, :], th[:, :], 0.1, 0.1, ALU.mult, ALU.add).then_inc(gth_done, 1)
                        dve.wait_ge(gth_done, count(s + 1))
                        dve.wait_ge(o_ready, count(s - 1))
                        nc.vector.tensor_tensor(
                            memo[par][:, :, :].rearrange("p (k h) d -> p k h d", k=KT),
                            Mb[0][:, P:2 * P].rearrange("p (k h d) -> p k h d", k=1, d=HD).broadcast_to([P, KT, NH, HD]),
                            gth[:, :].rearrange("p (k h d) -> p k h d", k=KT, d=1).broadcast_to([P, KT, NH, HD]),
                            op=ALU.mult).then_inc(memo_done, 1)
                    if f["attn"] and t in DVE_SLOT:
                        i = DVE_HEADS[DVE_SLOT.index(t)]
                        h = HEADS[i]
                        dve.wait_ge(exp_done, count(16 * a + i + 1))
                        nc.vector.tensor_tensor(probs[:, h, :], probs[:, h, :], decay_sb[:, :],
                                                op=ALU.mult).then_inc(mul_dve, 1)
                    if ffn == "on" and t == VE["ex_out"]:
                        c = s - FFN_AFTER
                        dve.wait_ge(fo_done, count(c + 1))
                        dve.wait_ge(ex_stored, count(16 * c))
                        nc.vector.tensor_tensor(
                            exout[:, :, :], Mb[0][:, :].rearrange("p (k d) -> p k d", d=D),
                            be_sb[:, ds(c * D, D)].rearrange("p (k d) -> p k d", k=1).broadcast_to([P, CK, D]),
                            op=ALU.add).then_inc(exout_done, 1)
                    if f["mx"] and t == VE["max1"]:
                        split_max(0)
                    if ffn == "over" and s in FINISHED and t == (0 if s == B + 1 else VE["finish"]):
                        tiles = GATHERS[s - 1]
                        dve.wait_ge(gathered[list(GATHERS).index(s - 1)], 16 * (tiles[1] - tiles[0]))
                        dve.wait_ge(y_done, count(s - 2))
                        finish(*FINISHED[s])
                    if f["fin"] and t == VE["wo"]:
                        dve.wait_ge(wo_done, count(o + 1))
                        dve.wait_ge(biased, 1)
                        xa = x_all[:, ds(o * KT, KT), :].rearrange("p k d -> p (k d)")
                        nc.vector.tensor_tensor(xa, Mb[1][:, 0:KT * D], xa, op=ALU.add).then_inc(y_done, 1)
                    if f["mx"] and t == RAW_FROM + 15:
                        split_max(1)
                    if f["pre"] and t == VE["cq"]:
                        dve.wait_ge(q_done, count(s + 3))
                        dve.wait_ge(qk_done, count(s + 2))
                        nc.vector.scalar_tensor_tensor(turn1[:, 0, :], Mb[1][:, 0:T], bq_sb[:, 0:1], cos_sb[:, :],
                                                       op0=ALU.add, op1=ALU.mult)
                        nc.vector.scalar_tensor_tensor(turn2[:, 0, :], Mb[1][:, T:2 * T], bqr_sb[:, 0:1], sin_sb[:, :],
                                                       op0=ALU.add, op1=ALU.mult).then_inc(q_rope, 1)
                    if f["pre"] and t == VE["k"]:
                        dve.wait_ge(k_done, count(s + 3))
                        nc.vector.tensor_tensor(turn1[:, 1, :], Mb[1][:, 0:T], cos_sb[:, :], op=ALU.mult)
                        nc.vector.tensor_tensor(turn2[:, 1, :], Mb[1][:, T:2 * T], sin_sb[:, :],
                                                op=ALU.mult).then_inc(k_rope, 1)

            seq = [0]

            def then(ins):
                seq[0] += 1
                ins.then_inc(rt, 1)
                dve.wait_ge(rt, seq[0])

            def route():

                def wide(v):
                    return v[:, :].unsqueeze(2).broadcast_to([P, NT, NE])

                def each(v):
                    return v[:, :].unsqueeze(1).broadcast_to([P, NT, NE])

                dve.wait_ge(w_late, 16 * 13)
                dve.wait_ge(lg_copied, NCH)
                then(nc.vector.tensor_reduce(top[:, :], logits[:, :, :], axis=AX.X, op=ALU.max))
                nc.vector.tensor_tensor(shifted[:, :, :], logits[:, :, :], wide(top), op=ALU.subtract).then_inc(rt_shift, 1)
                then(nc.vector.tensor_tensor(hit[:, :, :], logits[:, :, :], wide(top), op=ALU.is_equal))
                then(nc.vector.tensor_tensor(rank[:, :, :], hit[:, :, :], each(rank_sb), op=ALU.mult))
                then(nc.vector.tensor_reduce(toprank[:, :], rank[:, :, :], axis=AX.X, op=ALU.max))
                then(nc.vector.tensor_tensor(mask[:, :, :], rank[:, :, :], wide(toprank), op=ALU.is_equal))
                nc.vector.tensor_copy(maskb[:, :, :], mask[:, :, :]).then_inc(mask_done, 1)
                dve.wait_ge(rt_pe, 2)
                then(nc.vector.tensor_copy(pre[0][:, :, :], Xb[1][:, 0:NT * NE].rearrange("p (t e) -> p t e", e=NE)))
                for i in range(5):
                    d = 1 << i
                    nc.vector.tensor_copy(pre[i + 1][:, 0:d, :], pre[i][:, 0:d, :])
                    then(nc.vector.tensor_tensor(pre[i + 1][:, d:NT, :], pre[i][:, d:NT, :], pre[i][:, 0:NT - d, :], op=ALU.add))
                v = Xb[0][:, 0:NT * NE].rearrange("p (t e) -> p t e", e=NE)
                nc.vector.tensor_copy(where[:, 0:1, :], v[:, 0:1, :])
                then(nc.vector.tensor_tensor(where[:, 1:NT, :], v[:, 1:NT, :], pre[5][:, 0:NT - 1, :], op=ALU.add))
                then(nc.vector.tensor_tensor(picked[:, :, :], where[:, :, :], mask[:, :, :], op=ALU.mult))
                then(nc.vector.tensor_reduce(place[:, :], picked[:, :, :], axis=AX.X, op=ALU.add))
                then(nc.vector.tensor_tensor(based[:, :, :], mask[:, :, :], each(base_sb), op=ALU.mult))
                then(nc.vector.tensor_reduce(first[:, :], based[:, :, :], axis=AX.X, op=ALU.add))
                then(nc.vector.tensor_scalar(keep[:, :], place[:, :], float(CAP), None, ALU.is_lt))
                then(nc.vector.tensor_tensor(slot[:, :], first[:, :], place[:, :], op=ALU.add))
                then(nc.vector.tensor_tensor(kept_slot[:, :], slot[:, :], keep[:, :], op=ALU.mult))
                nc.vector.tensor_copy(src_u[:, :], kept_slot[:, :])
                then(nc.vector.tensor_tensor(off[:, :], slot[:, :], spare_sb[:, :], op=ALU.subtract))
                then(nc.vector.tensor_tensor(dest[:, :], off[:, :], keep[:, :], op=ALU.mult))
                then(nc.vector.tensor_tensor(dest2[:, :], dest[:, :], spare_sb[:, :], op=ALU.add))
                nc.vector.tensor_copy(dest_u[:, :], dest2[:, :]).then_inc(routed, 1)

            def gates():
                dve.wait_ge(rt_exp, 1)
                then(nc.vector.tensor_reduce(denom[:, :], expl[:, :, :], axis=AX.X, op=ALU.add))
                then(nc.vector.reciprocal(invden[:, :], denom[:, :]))
                then(nc.vector.tensor_tensor(gate[:, :], invden[:, :], keep[:, :], op=ALU.mult))

            def finish(first, last):
                for b in range(first, last):
                    for t in range(b * KT, b * KT + KT):
                        last_one = nc.vector.scalar_tensor_tensor(x_all[:, t, :], ffn_all[:, t, :], gate[:, t:t + 1],
                                                                  x_all[:, t, :], op0=ALU.mult, op1=ALU.add)
                    last_one.then_inc(res_done, 1)

            stats_of(0)
            normalise(0)
            normalise(1)
            stats_of(1)
            normalise(2)
            normalise(3)
            step(-2, 0, None, -1)
            logits_out(0)
            logits_out(1)
            normalise(4)
            normalise(5)
            step(-1, 1, None, -1)
            logits_out(2)
            logits_out(3)
            normalise(6)
            normalise(7)
            for c in range(4, NCH):
                logits_out(c)
            route()
            step(0, 0, None, 0)
            gates()
            run_steps(dve, step, from_step=1)
            dve.wait_ge(y_done, B)
            finish(B - 1, B)

        @block.tensor
        def _(pe):
            pe.wait_ge(w_early, 32)

            def turn_tokens(c):
                pe.wait_ge(xn_done, c + 1)
                pe.wait_ge(xT_evac, count(c - 1))
                for k in range(CK):
                    last = nc.tensor.transpose(Sb[c % 2][:, k * P:(k + 1) * P], xn_all[:, c * CK + k, :], id_sb[:, :])
                last.then_inc(xT_done, 1)

            def router(c):
                pe.wait_ge(xT_evac, c + 1)
                pe.wait_ge(lg_copied, count(c - 1))
                for k in range(CK):
                    t = c * CK + k
                    last = nc.tensor.matmul(Xb[c % 2][:, k * NE:(k + 1) * NE], xnT[:, t * P:(t + 1) * P], wg_sb[:, :],
                                            start=True, stop=True)
                last.then_inc(lg_done, 1)

            def step(s, par, ffn, u):
                f = has(s)
                other = 1 - par
                p, a, o = s + 2, s - 1, s - 2

                experts_now = count(s - FFN_AFTER + 1, NCH) if ffn == "on" else NCH if ffn == "over" else 0

                def pv(b, slot, g):
                    heads = HEADS[4 * g:4 * g + 4]
                    half, e = g // 2, g % 2
                    done = [i for i in range(NH) if i < 4 * g + 4]
                    pe.wait_ge(exp_done, count(b * NH + len(done)))
                    pe.wait_ge(mul_pool, count(pool_mults(b, len(done))))
                    pe.wait_ge(mul_dve, count(b * len(DVE_HEADS) + sum(i in DVE_HEADS for i in done)))
                    if e == 0:
                        pe.wait_ge(o_evac, count(2 * b + half))
                    for k in range(KT):
                        for j, h in enumerate(heads):
                            last = nc.tensor.matmul(PVb[32 * j:32 * j + 32, half * T:(half + 1) * T],
                                                    Va[slot][:, k, 32 * h:32 * h + 32],
                                                    probs[:, h, k * T:(k + 1) * T],
                                                    start=(e == 0 and k == 0), stop=(e == 1 and k == KT - 1))
                    last.then_inc(pv_done, 1)

                for t in range(SLOTS):
                    if f["attn"]:
                        for n in [n for n in range(NH) if SCORES[n] == t]:
                            e, g = n // GROUP, HEADS[n] % GROUP
                            if n % 8 == 0:
                                pe.wait_ge(mrow_in[n // 8], count(16 * (a + 1)))
                            pe.wait_ge(exp_done, count(16 * a + n - 1))
                            if n in log_heads(a):
                                for i in range(3):
                                    nc.tensor.matmul(Sb[n % 2][:, :], idb_sb[:, :], logd_sb[:, i * KT * T:(i + 1) * KT * T],
                                                     start=(i == 0), stop=False)
                            for k in range(KT):
                                last = nc.tensor.matmul(Sb[n % 2][:, k * T:(k + 1) * T],
                                                        Ks[other][e][:, g, k * P:(k + 1) * P], Qs[other][e][:, g, :],
                                                        start=n not in log_heads(a), stop=n not in log_heads(a) or k == KT - 1)
                            last.then_inc(s_done, 1)
                    if f["mx"] and RAW_FROM <= t < RAW_FROM + 16:
                        i = t - RAW_FROM
                        half, g, q = i // 8, i % 8 // 2 * 2, i % 2
                        if i == 0 and ffn is None:
                            pe.wait_ge(routed, 1)
                        if i % 8 == 0:
                            pe.wait_ge(stack_in[par][half], count(96 * (u + 1)))
                        pe.wait_ge(reduced, count(16 * s + i - 1))
                        for j in range(2):
                            last = nc.tensor.matmul(Xb[i % 2][:, j * T:(j + 1) * T], Qs[par][half][0:MROW, g + j, q * P:(q + 1) * P],
                                                    Ks[par][half][0:MROW, g + j, :], start=True, stop=True)
                        last.then_inc(raw_done, 1)
                    if f["attn"] and t == PE["max2"]:
                        pe.wait_ge(mt_evac, count(2 * s - 1, 2 * B))
                        pe.wait_ge(maxlo, count(2 * s))
                        for k in range(KT):
                            last = nc.tensor.transpose(Mb[2][0:16, k * P // 2:(k + 1) * P // 2].bitcast(bf16),
                                                       maxparts[:, k, 1, :], idb_sb[:, :])
                        last.then_inc(mt_done, 1)
                    if ffn == "on" and t == PE["ex_in"]:
                        pe.wait_ge(k_rope, count(s + 2, B))
                        pe.wait_ge(ex_in, count(16 * (s - FFN_AFTER + 1)))
                        for k in range(CK):
                            last = nc.tensor.transpose(Mb[1][:, k * P:(k + 1) * P], exin[:, k, :], id_sb[:, :])
                        last.then_inc(ft_done, 1)
                    if f["fin"] and t == PE["pv2"]:
                        pv(o, par, 3)
                    if f["fin"] and t == PE["o_turn"]:
                        pe.wait_ge(mt_evac, count(2 * s, 2 * B))
                        pe.wait_ge(o_evac, count(2 * o + 2))
                        for q in range(KT):
                            for half in range(2):
                                at = (2 * q + half) * P
                                last = nc.tensor.transpose(Mb[2][:, at:at + P], Oacc[:, half, q * P:(q + 1) * P], id_sb[:, :])
                        last.then_inc(otr_done, 1)
                    if f["mx"] and t == PE["mem"]:
                        pe.wait_ge(c_evac, count(s + 2, B))
                        pe.wait_ge(v_evac, count(s, B))
                        pe.wait_ge(mk_done, count(s + 1))
                        for k in range(KT):
                            nc.tensor.matmul(Mb[0][:, k * NH:(k + 1) * NH], qk[par][:, 0, k * P:(k + 1) * P], mk[par][:, :],
                                             start=True, stop=True)
                        pe.wait_ge(cmean_done, count(s + 1))
                        nc.tensor.matmul(Mb[0][:, P:2 * P], cmean[par][:, :], wv_sb[:, :], start=True,
                                         stop=True).then_inc(mem_done, 1)
                    if f["fin"] and t == PE["o_back"]:
                        pe.wait_ge(o_ready, count(o + 1))
                        for k in range(KT):
                            last = nc.tensor.transpose(Mb[2][:, k * P:(k + 1) * P],
                                                       Oq[:, k * NH:(k + 1) * NH, :].rearrange("p h d -> p (h d)"), id_sb[:, :])
                        last.then_inc(o2t_done, 1)
                    if ffn == "on" and t == PE["ex_out"]:
                        pe.wait_ge(memo_done, count(s + 1, B))
                        pe.wait_ge(ft_evac, s - FFN_AFTER + 1)
                        for k in range(CK):
                            last = nc.tensor.matmul(Mb[0][:, k * D:(k + 1) * D], exT[:, k * P:(k + 1) * P],
                                                    wet_sb[:, ds((s - FFN_AFTER) * D, D)], start=True, stop=True)
                        last.then_inc(fo_done, 1)
                    if f["mx"] and t == PE["values"]:
                        pe.wait_ge(memo_done, count(s + 1, B))
                        pe.wait_ge(exout_done, experts_now)
                        pe.wait_ge(c_evac, count(s + 1))
                        for k in range(KT):
                            last = nc.tensor.matmul(Mb[0][:, k * P:(k + 1) * P], cT[par][:, k * P:(k + 1) * P], wv_sb[:, :],
                                                    start=True, stop=True)
                        last.then_inc(v_done, 1)
                    if f["fin"] and t == PE["wo"]:
                        pe.wait_ge(k_rope, count(s + 2, B))
                        pe.wait_ge(ft_evac, experts_now)
                        pe.wait_ge(o2t_evac, count(o + 1))
                        for k in range(KT):
                            last = nc.tensor.matmul(Mb[1][:, k * D:(k + 1) * D], OT[:, k * P:(k + 1) * P], wo_sb[:, :],
                                                    start=True, stop=True)
                        last.then_inc(wo_done, 1)
                    if f["mx"] and t == PE["max1"]:
                        pe.wait_ge(mt_evac, count(2 * s, 2 * B))
                        pe.wait_ge(o2t_evac, count(s - 1, B))
                        pe.wait_ge(maxlo, count(2 * s + 1))
                        for k in range(KT):
                            last = nc.tensor.transpose(Mb[2][0:16, k * P // 2:(k + 1) * P // 2].bitcast(bf16),
                                                       maxparts[:, k, 0, :], idb_sb[:, :])
                        last.then_inc(mt_done, 1)
                    if f["pre"] and t == PE["cq"]:
                        xb = xnT[:, ds(p * T, T)]
                        pe.wait_ge(v_evac, count(s + 1, B))
                        pe.wait_ge(c_evac, count(s + 2, B))
                        nc.tensor.matmul(Mb[0][0:LAT, 0:T], wd_sb[:, :], xb, start=True, stop=True).then_inc(c_done, 1)
                        pe.wait_ge(k_rope, count(s + 2, B))
                        pe.wait_ge(y_done, count(s - 1, B))
                        nc.tensor.matmul(Mb[1][:, 0:T], wq_sb[:, :], xb, start=True, stop=True)
                        nc.tensor.matmul(Mb[1][:, T:2 * T], wqr_sb[:, :], xb, start=True, stop=True).then_inc(q_done, 1)
                    if f["pre"] and t == PE["k"]:
                        pe.wait_ge(q_rope, count(s + 3, B))
                        pe.wait_ge(c_evac, count(s + 3))
                        nc.tensor.matmul(Mb[1][:, 0:T], wk_sb[:, :], cT[par][:, :], start=True, stop=True)
                        nc.tensor.matmul(Mb[1][:, T:2 * T], wkr_sb[:, :], cT[par][:, :], start=True,
                                         stop=True).then_inc(k_done, 1)
                    if f["attn"] and t in PV_SLOT:
                        pv(a, other, PV_SLOT.index(t))

            def count_tokens():
                pe.wait_ge(mask_done, 1)
                pe.wait_ge(lg_copied, NCH)
                mb = maskb[:, :, :].rearrange("p t e -> p (t e)")
                nc.tensor.matmul(Xb[0][:, 0:NT * NE], before_sb[:, :], mb, start=True, stop=True).then_inc(rt_pe, 1)
                nc.tensor.matmul(Xb[1][:, 0:NT * NE], onesb_sb[:, :], mb, start=True, stop=True).then_inc(rt_pe, 1)

            turn_tokens(0)
            turn_tokens(1)
            router(0)
            pe.wait_ge(w_proj, 16 * 11)
            pe.wait_ge(init_dve, 1)
            pe.wait_ge(xT_evac, 1)
            step(-2, 0, None, -1)
            turn_tokens(2)
            router(1)
            turn_tokens(3)
            step(-1, 1, None, -1)
            for c in range(4, NCH):
                router(c - 2)
                turn_tokens(c)
            router(NCH - 2)
            router(NCH - 1)
            pe.wait_ge(init_pool, 2)
            pe.wait_ge(one_rows_in, 64)
            pe.wait_ge(w_late, 16 * 13)
            count_tokens()
            pe.wait_ge(xT_evac, NCH)
            run_steps(pe, step)


ROWS = np.arange(P).reshape(2, GROUP, HD).transpose(0, 2, 1).reshape(-1)


def _tables():
    bf = np.dtype("bfloat16")
    f = np.float32
    inv = (f(1.0) / np.power(f(10000.0), np.arange(0, HD, 2, dtype=f) / f(HD))).astype(f)
    freq = np.outer(np.arange(T, dtype=f), inv).astype(f)
    cos, sin = np.cos(freq).astype(f).T, np.sin(freq).astype(f).T
    rope_cos = np.tile(np.concatenate([cos, cos]), (NH, 1))[ROWS]
    rope_sin = np.tile(np.concatenate([-sin, sin]), (NH, 1))[ROWS]
    i = np.arange(T, dtype=np.float64)
    d = i[None, :] - i[:, None]
    dec = np.exp(-0.1 * np.log(np.abs(d) + 1.0)) * (np.exp(-np.maximum(d, 0.0) * 0.01) + 1e-9)
    rest, log_decay = (np.log(dec) / SCALE).reshape(KT, P, T).transpose(1, 0, 2).reshape(P, KT * T), []
    for _ in range(3):
        log_decay.append(rest.astype(bf))
        rest = rest - log_decay[-1].astype(np.float64)
    decay = dec.reshape(KT, P, T).transpose(1, 0, 2).reshape(P, KT * T)
    ident = np.eye(P)
    before = np.triu(np.ones((P, P)), 1)
    head_mean = np.repeat(np.eye(NH), HD, axis=0)[ROWS] / T
    one_rows = np.ones((2, GROUP * T))
    rank = np.tile(np.arange(NE, 0, -1.0), (P, 1))
    base = np.tile(np.arange(NE) * float(CAP), (P, 1))
    spare = NTOK + np.arange(NTOK, dtype=f).reshape(NT, P).T
    c = np.ascontiguousarray
    return [c(rope_cos, f), c(rope_sin, f), c(decay, f), np.concatenate(log_decay, 1), c(ident, f), c(ident).astype(bf), before.astype(bf),
            np.ones((P, P)).astype(bf), c(head_mean, f), one_rows.astype(bf),
            c(rank, f), c(base, f), c(spare, f)]


def kernel(**inputs):
    import concourse.bacc as _bacc
    from concourse import mybir as _mybir
    from concourse.bass_utils import run_bass_kernel_spmd as _run

    a = {k.replace("L0_", ""): np.asarray(v) for k, v in inputs.items()}
    swap = (np.arange(NH * HD).reshape(NH, 2, HD // 2)[:, ::-1]).reshape(-1)[ROWS]
    up = np.concatenate([a["attn_Wkv_up"], a["attn_bkv_up"][None, :]])
    up = up.reshape(LAT + 1, NH, 2, HD)
    wk, wv = up[:, :, 0].reshape(LAT + 1, P), up[:, :, 1].reshape(LAT + 1, P)
    wet = a["ffn_W"].transpose(2, 0, 1).reshape(D, NE * D)
    arrs = [a["attn_x"], a["attn_Wq"][:, ROWS], a["attn_Wq"][:, swap], a["attn_bq"][ROWS][:, None], a["attn_bq"][swap][:, None],
            a["attn_Wkv_down"], a["attn_bkv_down"][:, None], wk[:, ROWS], wk[:, swap], wv, a["attn_Wo"], a["attn_bo"][None, :],
            a["ffn_wg"], wet, a["ffn_b"].reshape(1, NE * D)] + _tables()
    names = ["x", "wq", "wqr", "bq", "bqr", "wd", "bd", "wk", "wkr", "wv", "wo", "bo", "wg", "wet", "be",
             "rope_cos", "rope_sin", "decay", "log_decay", "ident", "identb", "before", "onesb", "head_mean", "one_rows",
             "expert_rank", "expert_base", "spare_slot"]
    nc = _bacc.Bacc("TRN2", target_bir_lowering=False, num_devices=1)
    arrays, args = {}, []
    for name, v in zip(names, arrs):
        v = np.ascontiguousarray(v)
        arrays[f"in_{name}_dram"] = v
        args.append(nc.dram_tensor(f"in_{name}_dram", v.shape, _mybir.dt.from_np(v.dtype), kind="ExternalInput").ap())
    args.append(nc.dram_tensor("out_0_dram", (B, T, D), _mybir.dt.float32, kind="ExternalOutput").ap())
    mixed_block_kernel(nc, *args)
    r = _run(nc, [arrays], core_ids=[0])
    return r.results[0]["out_0_dram"]
```
